# Optimizing a Trainium2 kernel written in Bass

```python
import numpy as np
import jax
import jax.numpy as jnp

def _softmax(x, axis=-1):
    return jax.nn.softmax(x, axis=axis)

def _gelu(x):
    return jax.nn.gelu(x, approximate=True)

def _silu(x):
    return jax.nn.silu(x)

def _sigmoid(x):
    return jax.nn.sigmoid(x)

def _layernorm(x, axis=-1, eps=1e-05):
    m = jnp.mean(x, axis=axis, keepdims=True)
    v = jnp.var(x, axis=axis, keepdims=True)
    return (x - m) / jnp.sqrt(v + eps)

def _scatter_add(tgt, idx, src, axis=0):
    return tgt.at[idx].add(src)

def _segment_sum(src, seg, n):
    return jax.ops.segment_sum(src, seg, n)
kernel_name = 'mk_xattn_seq_d1_seqx_r2_fdf5a8'

def setup_inputs(seed: int=0):
    np.random.seed(seed)
    _w = jnp.asarray

    def _rec_inputs():
        import jax
        import jax.numpy as jnp
        _rk = jax.random.key(seed)
        x = -0.0002928 + 1 * jax.random.normal(jax.random.fold_in(_rk, 1), (2, 2048, 512), jnp.float32)
        _lenS = 2048 - jax.random.randint(jax.random.fold_in(_rk, 7), (2,), 0, max(1, 2048 // 4) + 1, jnp.int32)
        _lenS2 = 77 - jax.random.randint(jax.random.fold_in(_rk, 8), (2,), 0, max(1, 77 // 4) + 1, jnp.int32)
        _ctx_1024P = jax.random.normal(jax.random.fold_in(_rk, 11), (2, 16, 512), jnp.float32)
        _ctx_1024c = jax.random.dirichlet(jax.random.fold_in(_rk, 511), 0.3 * jnp.ones((16,), jnp.float32), (2, 77))
        _ctx_1024t = jnp.einsum('bsk,bkd->bsd', _ctx_1024c, _ctx_1024P)
        _ctx_1024t = _ctx_1024t * jax.lax.rsqrt(jnp.mean(jnp.square(_ctx_1024t)) + 1e-12) * 0.953939
        ctx_1024 = -1.39393e-06 + 0.999914 * (_ctx_1024t + 0.3 * jax.random.normal(jax.random.fold_in(_rk, 611), (2, 77, 512), jnp.float32))
        _validS = jnp.arange(2048)[None, :] < _lenS[:, None]
        _validS2 = jnp.arange(77)[None, :] < _lenS2[:, None]
        _causal = jnp.tril(jnp.ones((2048, 2048), dtype=bool))
        mask_BxSxS2_bk0 = jnp.logical_not(jnp.broadcast_to(_validS2[:, None, :], (2, 2048, 77)))
        return (x, ctx_1024, mask_BxSxS2_bk0)
    x, ctx_1024, mask_BxSxS2_bk0 = _rec_inputs()

    def _L0_xattn_setup():
        import jax, jax.numpy as jnp
        import numpy as np
        EPS = 1e-05

        def layer_norm(x, w, b):
            mu = jnp.mean(x, axis=-1, keepdims=True)
            var = jnp.var(x, axis=-1, keepdims=True)
            return (x - mu) * jax.lax.rsqrt(var + EPS) * w + b
        key = jax.random.key(seed)
        ks = jax.random.split(key, 12)
        B, N, M, C = (2, 1024, 1024, 512)
        H = 16
        hid = 4 * C
        s = lambda d: 1.0 / np.sqrt(d)
        return {'x': jax.random.normal(ks[0], (B, N, C), jnp.float32), 'context': jax.random.normal(ks[1], (B, M, C), jnp.float32), 'xa_mask': jax.random.bernoulli(ks[2], 0.1, (B, N, M)), 'qn_w': jnp.ones((C,), jnp.float32), 'qn_b': jnp.zeros((C,), jnp.float32), 'cn_w': jnp.ones((C,), jnp.float32), 'cn_b': jnp.zeros((C,), jnp.float32), 'n2_w': jnp.ones((C,), jnp.float32), 'n2_b': jnp.zeros((C,), jnp.float32), 'q_w': jax.random.normal(ks[3], (C, C), jnp.float32) * s(C), 'kv_w': jax.random.normal(ks[4], (C, 2 * C), jnp.float32) * s(C), 'proj_w': jax.random.normal(ks[5], (C, C), jnp.float32) * s(C), 'proj_b': jnp.zeros((C,), jnp.float32), 'fc1_w': jax.random.normal(ks[6], (C, hid), jnp.float32) * s(C), 'fc1_b': jnp.zeros((hid,), jnp.float32), 'fc2_w': jax.random.normal(ks[7], (hid, C), jnp.float32) * s(hid), 'fc2_b': jnp.zeros((C,), jnp.float32)}
    _L0_xattn_all = _L0_xattn_setup()
    _L0_xattn_in = {k: v for k, v in _L0_xattn_all.items() if k in ('qn_w', 'qn_b', 'cn_w', 'cn_b', 'n2_w', 'n2_b', 'q_w', 'kv_w', 'proj_w', 'proj_b', 'fc1_w', 'fc1_b', 'fc2_w', 'fc2_b')}
    del _L0_xattn_all
    return {'x': x, 'ctx_1024': ctx_1024, 'mask_BxSxS2_bk0': mask_BxSxS2_bk0, 'L0_xattn_qn_w': _L0_xattn_in['qn_w'], 'L0_xattn_qn_b': _L0_xattn_in['qn_b'], 'L0_xattn_cn_w': _L0_xattn_in['cn_w'], 'L0_xattn_cn_b': _L0_xattn_in['cn_b'], 'L0_xattn_n2_w': _L0_xattn_in['n2_w'], 'L0_xattn_n2_b': _L0_xattn_in['n2_b'], 'L0_xattn_q_w': _L0_xattn_in['q_w'], 'L0_xattn_kv_w': _L0_xattn_in['kv_w'], 'L0_xattn_proj_w': _L0_xattn_in['proj_w'], 'L0_xattn_proj_b': _L0_xattn_in['proj_b'], 'L0_xattn_fc1_w': _L0_xattn_in['fc1_w'], 'L0_xattn_fc1_b': _L0_xattn_in['fc1_b'], 'L0_xattn_fc2_w': _L0_xattn_in['fc2_w'], 'L0_xattn_fc2_b': _L0_xattn_in['fc2_b']}

def reference(x, ctx_1024, mask_BxSxS2_bk0, L0_xattn_qn_w, L0_xattn_qn_b, L0_xattn_cn_w, L0_xattn_cn_b, L0_xattn_n2_w, L0_xattn_n2_b, L0_xattn_q_w, L0_xattn_kv_w, L0_xattn_proj_w, L0_xattn_proj_b, L0_xattn_fc1_w, L0_xattn_fc1_b, L0_xattn_fc2_w, L0_xattn_fc2_b):
    import jax
    import jax.numpy as jnp

    def _L0_xattn_ref(x, context, xa_mask, qn_w, qn_b, cn_w, cn_b, n2_w, n2_b, q_w, kv_w, proj_w, proj_b, fc1_w, fc1_b, fc2_w, fc2_b):
        import jax, jax.numpy as jnp
        import numpy as np
        EPS = 1e-05

        def layer_norm(x, w, b):
            mu = jnp.mean(x, axis=-1, keepdims=True)
            var = jnp.var(x, axis=-1, keepdims=True)
            return (x - mu) * jax.lax.rsqrt(var + EPS) * w + b
        B, N, C = x.shape
        M = context.shape[1]
        H = 16
        D = C // H
        scale = D ** (-0.5)
        xq = layer_norm(x, qn_w, qn_b)
        ctx = layer_norm(context, cn_w, cn_b)
        q = (xq @ q_w).reshape(B, N, H, D)
        kv = (ctx @ kv_w).reshape(B, M, 2, H, D)
        k, v = (kv[:, :, 0], kv[:, :, 1])
        attn = jnp.einsum('bnhd,bmhd->bhnm', q, k) * scale
        neg = -jnp.finfo(attn.dtype).max
        attn = jnp.where(xa_mask[:, None, :, :], neg, attn)
        attn = jax.nn.softmax(attn, axis=-1)
        out = jnp.einsum('bhnm,bmhd->bnhd', attn, v).reshape(B, N, C)
        out = out @ proj_w + proj_b
        x = x + out
        h = layer_norm(x, n2_w, n2_b)
        h = jax.nn.gelu(h @ fc1_w + fc1_b, approximate=False) @ fc2_w + fc2_b
        return x + h
    x = _L0_xattn_ref(x, ctx_1024, mask_BxSxS2_bk0, L0_xattn_qn_w, L0_xattn_qn_b, L0_xattn_cn_w, L0_xattn_cn_b, L0_xattn_n2_w, L0_xattn_n2_b, L0_xattn_q_w, L0_xattn_kv_w, L0_xattn_proj_w, L0_xattn_proj_b, L0_xattn_fc1_w, L0_xattn_fc1_b, L0_xattn_fc2_w, L0_xattn_fc2_b)
    return x

_drawn_inputs = setup_inputs


def setup_inputs(seed=0):
    import zlib

    import numpy as np

    out = dict(_drawn_inputs(seed))
    spreads = {'L0_xattn_qn_w': (1.0, 0.2),
     'L0_xattn_qn_b': (0.0, 0.401),
     'L0_xattn_cn_w': (1.0, 0.2),
     'L0_xattn_cn_b': (0.0, 0.1),
     'L0_xattn_n2_w': (1.0, 0.2),
     'L0_xattn_n2_b': (0.0, 0.1),
     'L0_xattn_proj_b': (0.0, 0.1),
     'L0_xattn_fc1_b': (0.0, 0.1),
     'L0_xattn_fc2_b': (0.0, 0.1)}
    factors = {}
    for name, (base, spread) in spreads.items():
        noise = np.random.default_rng([zlib.crc32(name.encode()), seed]).standard_normal(out[name].shape)
        drawn = base * np.exp(spread * noise) if base else spread * noise
        out[name] = jnp.asarray(drawn.astype(out[name].dtype))
    for name, factor in factors.items():
        out[name] = (out[name] * factor).astype(out[name].dtype)
    return out
```

```python
import concourse.bass as bass
from concourse import mybir

F32 = mybir.dt.float32
F32R = mybir.dt.float32r
U8 = mybir.dt.uint8
ALU = mybir.AluOpType
ACT = mybir.ActivationFunctionType
AX = mybir.AxisListType

P = 128
EPS = 1e-5
FLT_MAX = 3.4028234663852886e38
HI, LO = 0, 1
PRODUCTS = ((HI, HI), (LO, HI), (HI, LO))


class Unit:

    def __init__(self, q, u):
        self.q, self.u = q, u

    def plus(self, d):
        return Unit(self.q + (self.u + d) // 2, (self.u + d) % 2)

    def slot(self):
        return (self.q % 2) * 2 + self.u


class Count:

    def __init__(self, nc, name, per, start=0):
        self.sem, self.per, self.start = nc.alloc_semaphore(name), per, start

    def after(self, unit, i):
        return unit.q * (2 * self.per) + (unit.u * self.per + self.start + i + 1)

    def wait(self, eng, unit, i):
        value = self.after(unit, i)
        if isinstance(value, int) and value <= self.start:
            return
        eng.wait_ge(self.sem, value)


def build_block(nc, x, ctx, mask, qn_w, qn_b, cn_w, cn_b, n2_w, n2_b, q_w, kv_w, proj_w, proj_b,
                fc1_w, fc1_b, fc2_w, fc2_b, out):
    B, N, C = x.shape
    M = ctx.shape[1]
    HID = fc1_w.shape[1]
    H = 16
    D = C // H
    SCALE = D ** -0.5
    KT = C // P
    HG = P // D
    GM = HG * M
    UT = 2
    UN = UT * P
    NU = B * N // UN
    NC = -(-GM // P)
    CH0 = [c * (GM - P) // (NC - 1) for c in range(NC)]
    CH0[-1] = GM - P
    SB = 512
    ST = SB // P
    NS = B * N // SB
    JT = HID // P
    assert B == 2 and N % UN == 0 and NU % 2 == 0 and NU >= 8 and NS % 2 == 0 and NS >= 4

    x_v = x.rearrange("b (n t p) c -> b p n t c", t=UT, p=P)
    mask_v = mask.rearrange("b (n t p) m -> b p n t m", t=UT, p=P)
    x2_dram = nc.dram_tensor("x2_scratch", [B * N, C], F32, kind="Internal").ap()
    x2_units = x2_dram.rearrange("(b n t p) c -> b p n t c", b=B, t=UT, p=P)
    x2_blocks = x2_dram.rearrange("(s t p) c -> p s t c", t=ST, p=P)
    out_blocks = out.rearrange("b n c -> (b n) c").rearrange("(s t p) c -> p s t c", t=ST, p=P)
    fc1_v = fc1_w.rearrange("(k p) (j n) -> j p k n", p=P, n=P)
    fc2_v = fc2_w.rearrange("(j p) n -> j p n", p=P)

    base = 16512
    top = [base]

    def at(name, shape, dt, offset=None):
        size = 1 if dt is U8 else 4
        for s in shape[1:]:
            size *= s
        if offset is None:
            offset = top[0]
            top[0] += (size + 31) // 32 * 32
        return nc.alloc_sbuf_tensor_at(name, shape, dt, offset=offset)

    ident = at("ident", [P, P], F32)
    cols = at("cols", [P, 40], F32)
    fc1_bias = at("fc1_bias", [P, JT], F32)
    qbias = at("qbias", [P, KT], F32)
    mhalf = at("mhalf", [P, 4], F32)
    wscale = at("wscale", [P, KT], F32)
    region1 = top[0]

    wq = [at(f"wq{s}", [P, KT, C], F32R) for s in "hl"]
    kbd = [at(f"kbd{s}", [P, B, KT, GM], F32R) for s in "hl"]
    xT = [at(f"xT{s}", [P, KT, UN], F32R) for s in "hl"]
    qT = [at(f"qT{s}", [P, KT, UN], F32R) for s in "hl"]
    xhat = at("xhat", [P, UT, C], F32)
    wp = [at(f"wp{s}", [P, KT, C], F32R) for s in "hl"]
    vbd = [at(f"vbd{s}", [P, B, KT * NC, P], F32R) for s in "hl"]
    S = at("S", [P, 2, UT, H * M], F32)
    PT = [at(f"PT{s}", [P, 2, NC, UN], F32R) for s in "hl"]
    aT = [at(f"aT{s}", [P, KT, UN], F32R) for s in "hl"]
    xr = at("xr", [P, 4, UT, C], F32)
    projb = at("projb", [P, C], F32)
    mask_in = at("mask_in", [P, 2, UT, M], U8)
    negm = at("negm", [P, 2, UT, M], F32)
    bnst = at("bnst", [P, UT, 6], F32)
    mv = at("mv", [P, UT, 2], F32)
    veps = at("veps", [P, UT], F32)
    rstd = at("rstd", [P, UT], F32)
    nmax = at("nmax", [P, 2, UT, H], F32)
    esum = at("esum", [P, 2, UT, H], F32)
    rsum = at("rsum", [P, 2, UT, H], F32)
    region2 = top[0]

    kvw = at("kvw", [P, KT, 2 * C], F32)
    qraw = at("qraw", [P, KT, C], F32)
    praw = at("praw", [P, KT, C], F32)
    cx = at("cx", [P, B, C], F32)
    cxT = at("cxT", [P, KT, B, M], F32)
    vtok = [at(f"vtok{s}", [P, B, C], F32R) for s in "hl"]
    rows = at("rows", [40, P], F32)
    cbn = at("cbn", [P, B, 6], F32)
    cmv = at("cmv", [P, B, 2], F32)
    cve = at("cve", [P, B], F32)
    crs = at("crs", [P, B], F32)
    end0 = top[0]

    top[0] = region2
    x2_0 = at("x2_0", [P, ST, C], F32)
    hT_0 = [at(f"hT0{s}", [P, KT, SB], F32R) for s in "hl"]
    w1raw = at("w1raw", [P, 2, KT, P], F32)
    w2raw = at("w2raw", [P, C], F32)
    fc2b = at("fc2b", [P, C], F32)
    g = at("g", [P, SB], F32)
    gT = [at(f"gT{s}", [P, 4, SB], F32R) for s in "hl"]
    hbn = at("hbn", [P, 6], F32)
    hmv = at("hmv", [P, 2], F32)
    hve = at("hve", [P, 1], F32)
    hrs = at("hrs", [P, 1], F32)
    end2 = top[0]
    top[0] = region1
    w1 = at("w1", [P, JT, 2, KT, P], F32R)
    w2 = at("w2", [P, JT, 2, C], F32R)
    x2_1 = at("x2_1", [P, ST, C], F32)
    hT_1 = [at(f"hT1{s}", [P, KT, SB], F32R) for s in "hl"]
    hhat = at("hhat", [P, C], F32)
    assert top[0] <= region2 and max(end0, end2) <= 229344, (top[0], region2, end0, end2)
    x2 = [x2_0, x2_1]
    hT = [hT_0, hT_1]

    QNW, QNB, CNW, CNB, N2W, N2B, F1B = (4 * i for i in range(7))

    bank = [nc.alloc_psum_tensor(f"bank{i}", [P, 512], F32) for i in range(8)]
    bA, bS, bT, bV = bank[0:2], bank[2:4], bank[4:6], bank[6:8]
    bC, bF, bX, bB = bank[0:4], bank[4:6], bank[6], bank[7]

    def sem(name):
        return nc.alloc_semaphore(name)

    d_rows, d_ctx, d_kvw, d_qw, d_pw, d_projb, d_vbd = (sem(f"d_{n}") for n in
                                                         ("rows", "ctx", "kvw", "qw", "pw", "projb", "vbd"))
    d_x = [sem("d_x0"), sem("d_x1")]
    d_mask = [sem("d_mask0"), sem("d_mask1")]
    d_x2st = sem("d_x2st")
    p_ident, p_half, p_zero, p_crs = sem("p_ident"), sem("p_half"), sem("p_zero"), sem("p_crs")
    v_set, t_set = sem("v_set"), sem("t_set")

    def count(name, per, start=0):
        return Count(nc, name, per, start)

    t_scores = count("t_scores", UT * KT)
    v_scores = count("v_scores", UT * KT, 2)
    v_max = count("v_max", UT)
    a_exp = count("a_exp", UT)
    v_rsum = count("v_rsum", UT)
    p_prob = count("p_prob", UT)
    t_probT = count("t_probT", KT * UT, 1)
    a_probT = count("a_probT", KT * UT)
    v_probT = count("v_probT", KT * UT, 2)
    t_av = count("t_av", KT, 2)
    a_av = count("a_av", KT)
    v_av = count("v_av", KT)
    t_proj = count("t_proj", UT, 1)
    v_res = count("v_res", UT, 2)
    t_xT = count("t_xT", UT)
    a_xT = count("a_xT", UT)
    v_xT = count("v_xT", UT)
    t_q = count("t_q", UT, 1)
    a_q = count("a_q", UT)
    v_q = count("v_q", UT, 2)
    v_bn, v_mv, v_veps = count("v_bn", UT), count("v_mv", UT), count("v_veps", 1)
    p_rstd = count("p_rstd", 1)
    v_xhat = count("v_xhat", UT)
    p_projb = count("p_projb", UT)
    p_neg = count("p_neg", 1)
    counts1 = [v_scores, t_probT, v_probT, t_av, t_proj, v_res, t_q, v_q]

    d_w1 = [sem("d_w1_0"), sem("d_w1_1")]
    d_w2 = sem("d_w2")
    d_fc2b, d_out = sem("d_fc2b"), sem("d_out")
    d_x2 = [sem("d_x2_0"), sem("d_x2_1")]
    t_bias, v_bias, p_w1, a_w1, v_w1, a_w2, v_w2 = (sem(n) for n in
                                                    ("t_bias", "v_bias", "p_w1", "a_w1", "v_w1", "a_w2", "v_w2"))
    v_hbn, v_hmv, v_hve = count("v_hbn", ST), count("v_hmv", ST), count("v_hve", ST)
    p_hrs, v_hhat = count("p_hrs", ST), count("v_hhat", ST)
    t_hT, a_hT, v_hT = count("t_hT", ST), count("a_hT", ST), count("v_hT", ST)
    t_fc1 = count("t_fc1", JT)
    a_gelu = count("a_gelu", JT)
    v_ghi = count("v_ghi", JT)
    v_glo = count("v_glo", JT)
    t_fc2 = count("t_fc2", JT * ST)
    v_out = count("v_out", ST)
    p_fc2b = count("p_fc2b", ST)

    def f32(ap):
        return ap.bitcast(F32)

    def units(lo, hi, eng, body):
        with eng.Fori(lo // 2, hi // 2) as q:
            for u in range(2):
                body(Unit(q, u))

    def static(n):
        return Unit(n // 2, n % 2)

    LOOP = (0, (NU - 4) // 2 * 2)

    def pipeline(eng, step):
        step(static(-3), norm=True)
        step(static(-2), front=True, norm=True)
        step(static(-1), scores=True, front=True, norm=True)
        units(*LOOP, eng, lambda k: step(k, back=True, scores=True, front=True, norm=True))
        for n in range(LOOP[1], NU):
            step(static(n), back=True, scores=n + 1 < NU, front=n + 2 < NU, norm=n + 3 < NU)

    NORMS = [5 + 2 * t for t in range(ST)]
    assert NORMS[-1] + 2 < JT

    def blocks(eng, step):
        step(static(0), first=True)
        with eng.Fori(0, (NS - 2) // 2) as i:
            step(Unit(i, 1))
            step(Unit(i + 1, 0))
        step(static(NS - 1), last=True)

    last = static(NU - 1)
    s_chain = sem("v_chain")

    def sync_program(sp):
        def load_x(n):
            sp.dma_start(xr[:, bass.ds(n.slot(), 1), :, :],
                         x_v[n.u][:, bass.ds(n.q, 1), :, :]).then_inc(d_x[n.u], 16)

        def load_mask(n):
            sp.dma_start(mask_in[:, n.u:n.u + 1, :, :],
                         mask_v[n.u][:, bass.ds(n.q, 1), :, :]).then_inc(d_mask[n.u], 16)

        for i, v in enumerate((qn_w, qn_b, cn_w, cn_b, n2_w, n2_b)):
            sp.dma_start(rows[4 * i:4 * i + 4, :], v.rearrange("(k p) -> k p", p=P)).then_inc(d_rows, 16)
        sp.dma_start(rows[24:40, :], fc1_b.rearrange("(k p) -> k p", p=P)).then_inc(d_rows, 16)
        load_x(static(0))
        load_x(static(1))
        load_mask(static(0))
        load_mask(static(1))
        for n in (2, 3):
            sp.wait_ge(d_x[n % 2], 16)
            load_x(static(n))
        sp.dma_start(projb[:, :], proj_b.rearrange("(a c) -> a c", a=1).to_broadcast([P, C])).then_inc(d_projb, 16)
        sp.wait_ge(v_set, 8)
        sp.wait_ge(p_zero, 4)
        for part, b, h, c in ((part, b, h, c) for part in (HI, LO) for b in range(B) for h in range(HG) for c in range(NC)):
            own = 0 if c == 0 else CH0[c - 1] + P
            r0, r1 = max(h * M, own), min((h + 1) * M, CH0[c] + P)
            if r0 < r1:
                sp.dma_start(
                    f32(vbd[part][r0 - CH0[c]:r1 - CH0[c], b, :, :]).rearrange("p (g c) n -> p g c n", c=NC)[
                        :, :, c, h * D:(h + 1) * D],
                    f32(vtok[part][r0 - h * M:r1 - h * M, b, :]).rearrange("p (g n) -> p g n", g=KT)[
                        :, :, h * D:(h + 1) * D]).then_inc(d_vbd, 16)
        for n in (2, 3):
            p_neg.wait(sp, static(n - 2), 0)
            load_mask(static(n))

        def step(k, more=True):
            v_res.wait(sp, k, UT - 1)
            sp.dma_start(x2_units[k.u][:, bass.ds(k.q, 1), :, :],
                         xr[:, bass.ds(k.slot(), 1), :, :]).then_inc(d_x2st, 16)
            if more:
                sp.wait_ge(d_x2st, k.q * 32 + (k.u * 16 + 16))
                load_x(k.plus(4))
                load_mask(k.plus(4))

        units(0, NU - 4, sp, step)
        for n in range(NU - 4, NU):
            step(static(n), more=False)

        def load_w(j):
            b = j % 2
            if j >= 2:
                sp.wait_ge(v_w1, j - 1)
            sp.dma_start(w1raw[:, b, :, :], fc1_v[j]).then_inc(d_w1[b], 16)
            if j >= 1:
                sp.wait_ge(v_w2, j)
            sp.dma_start(w2raw[:, :], fc2_v[j]).then_inc(d_w2, 16)

        def load_x2(s):
            sp.dma_start(x2[s.u][:, :, :].unsqueeze(1), x2_blocks[:, bass.ds(s.q * 2 + s.u, 1), :, :]).then_inc(d_x2[s.u], 16)

        def store_out(s):
            v_out.wait(sp, s, ST - 1)
            sp.dma_start(out_blocks[:, bass.ds(s.q * 2 + s.u, 1), :, :], x2[s.u][:, :, :].unsqueeze(1)).then_inc(d_out, 16)
            sp.wait_ge(d_out, s.q * 32 + (s.u * 16 + 16))

        sp.wait_ge(d_x2st, 16 * NU)
        sp.dma_start(fc2b[:, :], fc2_b.rearrange("(a c) -> a c", a=1).to_broadcast([P, C])).then_inc(d_fc2b, 16)
        load_x2(static(0))
        t_proj.wait(sp, last, UT - 1)
        load_x2(static(1))
        for j in range(JT):
            load_w(j)
        store_out(static(0))
        load_x2(static(2))
        with sp.Fori(0, (NS - 2) // 2 - 1) as i:
            for s in (Unit(i, 1), Unit(i + 1, 0)):
                store_out(s)
                load_x2(s.plus(2))
        store_out(static(NS - 3))
        load_x2(static(NS - 1))
        store_out(static(NS - 2))
        store_out(static(NS - 1))

    def gpsimd_program(pool):
        pool.memset(mhalf[:, :], -0.5).then_inc(p_half, 1)
        pool.memset(ident[:, :], 0.0).then_inc(p_ident, 1)
        pool.wait_ge(p_ident, 1)
        pool.affine_select(out=ident[:, :], in_=ident[:, :], compare_op=ALU.not_equal, fill=1.0, base=0,
                           pattern=[[-1, P]], channel_multiplier=1).then_inc(p_ident, 1)
        for t in (*kbd, *vbd):
            pool.memset(f32(t[:, :, :, :]).rearrange("p a b c -> p (a b c)"), 0.0).then_inc(p_zero, 1)
        pool.wait_ge(p_half, 1)

        def power(dst, src, n):
            return pool.tensor_tensor(dst, src, mhalf[0:n, 0:src.shape[1]], ALU.pow)

        pool.wait_ge(v_set, 2)
        power(crs[0:M, :], cve[0:M, :], M).then_inc(p_crs, 1)

        def may_negate(n):
            pool.wait_ge(d_mask[n.u], n.q * 16 + 16)
            v_scores.wait(pool, n.plus(-2), UT * KT - 1)

        def negative(n):
            pool.tensor_scalar(negm[:, n.u, :, :], mask_in[:, n.u, :, :], -FLT_MAX, 1.0, ALU.mult,
                               ALU.mult).then_inc(p_neg.sem, 1)

        def step(k, back=False, scores=False, front=False, norm=False):
            if front:
                may_negate(k.plus(2))
            if norm:
                n = k.plus(3)
                v_veps.wait(pool, n, 0)
                v_xhat.wait(pool, n.plus(-1), UT - 1)
                power(rstd[:, :], veps[:, :], P).then_inc(p_rstd.sem, 1)
            if front:
                negative(k.plus(2))
            if back:
                for t in range(UT):
                    v = xr[:, bass.ds(k.slot(), 1), t, :]
                    pool.tensor_tensor(v, v, projb[:, :].unsqueeze(1), ALU.add).then_inc(p_projb.sem, 1)
            if scores:
                n = k.plus(1)
                for t in range(UT):
                    v_rsum.wait(pool, n, t)
                    v = S[:, n.u, t, :].rearrange("p (h m) -> p h m", h=H)
                    pool.tensor_tensor(v, v, rsum[:, n.u, t, :].unsqueeze(2).to_broadcast([P, H, M]),
                                       ALU.mult).then_inc(p_prob.sem, 1)

        pool.wait_ge(d_projb, 16)
        pipeline(pool, step)

        pool.wait_ge(d_fc2b, 16)

        def step2(s, first=False, last=False):
            def norm(n, t):
                v_hve.wait(pool, n, t)
                power(hrs[:, :], hve[:, :], P).then_inc(p_hrs.sem, 1)

            def bias(n, t):
                v_hhat.wait(pool, n, t)
                v = x2[n.u][:, t, :]
                pool.tensor_tensor(v, v, fc2b[:, :], ALU.add).then_inc(p_fc2b.sem, 1)

            def scale(j):
                pool.wait_ge(t_bias, j + 1)
                for k in range(KT):
                    v = w1raw[:, j % 2, k, :]
                    i = pool.tensor_scalar(v, v, cols[:, N2W + k:N2W + k + 1], 1.0, ALU.mult, ALU.mult)
                i.then_inc(p_w1, 1)

            if first:
                for t in range(ST):
                    norm(s, t)
                for t in range(ST):
                    bias(s, t)
                scale(0)
                scale(1)
            for j in range(JT):
                if first and j + 2 < JT:
                    scale(j + 2)
                if not last and j in NORMS:
                    norm(s.plus(1), NORMS.index(j))
                    bias(s.plus(1), NORMS.index(j))

        blocks(pool, step2)

    def scalar_program(act):
        act.dma_start(cx[0:M, :, :], ctx.rearrange("b m c -> m b c")).then_inc(d_ctx, 16)
        act.dma_start(kvw[:, :, :], kv_w.rearrange("(k p) n -> p k n", p=P)).then_inc(d_kvw, 16)
        act.dma_start(qraw[:, :, :], q_w.rearrange("(k p) n -> p k n", p=P)).then_inc(d_qw, 16)
        act.dma_start(praw[:, :, :], proj_w.rearrange("(k p) n -> p k n", p=P)).then_inc(d_pw, 16)

        def step(k, back=False, scores=False, front=False, norm=False):
            b, s, f = k, k.plus(1), k.plus(2)

            def x_hi(t):
                t_xT.wait(act, f, t)
                t_q.wait(act, f.plus(-1), UT - 1)
                act.activation(xT[HI][:, :, t * P:(t + 1) * P], bA[t][:, :].rearrange("p (k n) -> p k n", k=KT),
                               ACT.Copy).then_inc(a_xT.sem, 1)

            def q_hi(h):
                t_q.wait(act, f, h)
                for m in (2 * h, 2 * h + 1):
                    i = act.activation(qT[HI][:, m, :], bA[h][:, (m % 2) * UN:(m % 2 + 1) * UN], ACT.Identity,
                                       bias=qbias[:, m:m + 1])
                i.then_inc(a_q.sem, 1)

            def prob_hi(g_):
                for t in range(UT):
                    i = g_ * UT + t
                    if t == 0:
                        t_av.wait(act, b, g_ - 2)
                    t_probT.wait(act, b, i)
                    act.activation(PT[HI][:, g_ % 2, :, t * P:(t + 1) * P],
                                   bT[i % 2][:, 0:NC * P].rearrange("p (c n) -> p c n", c=NC),
                                   ACT.Copy).then_inc(a_probT.sem, 1)

            def av_hi(g_):
                if g_ == 0:
                    t_proj.wait(act, b.plus(-1), UT - 1)
                t_av.wait(act, b, g_)
                act.activation(aT[HI][:, g_, :], bV[g_ % 2][:, 0:UN], ACT.Copy).then_inc(a_av.sem, 1)

            def exps(t, lo, hi):
                if lo == 0:
                    v_max.wait(act, s, t)
                for h in range(lo, hi):
                    v = S[:, s.u, t, h * M:(h + 1) * M]
                    i = act.activation(v, v, ACT.Exp, bias=nmax[:, s.u, t, h:h + 1],
                                       accum_out=esum[:, s.u, t, h:h + 1])
                if hi == H:
                    i.then_inc(a_exp.sem, 1)

            if front:
                x_hi(0)
                x_hi(1)
            if back:
                prob_hi(0)
            if scores:
                exps(0, 0, 4)
            if back:
                prob_hi(1)
            if scores:
                exps(0, 4, 8)
            if back:
                av_hi(0)
            if front:
                q_hi(0)
            if scores:
                exps(0, 8, 12)
            if back:
                prob_hi(2)
                av_hi(1)
            if scores:
                exps(0, 12, 16)
            if back:
                prob_hi(3)
            if scores:
                exps(1, 0, 4)
            if back:
                av_hi(2)
            if front:
                q_hi(1)
            if back:
                av_hi(3)
            if scores:
                exps(1, 4, 16)

        pipeline(act, step)

        def step2(s, first=False, last=False):
            def split_hi(j):
                act.wait_ge(p_w1, j + 1)
                act.activation(w1[:, j, HI, :, :], w1raw[:, j % 2, :, :], ACT.Copy).then_inc(a_w1, 1)
                act.wait_ge(d_w2, 16 * j + 16)
                act.activation(w2[:, j, HI, :], w2raw[:, :], ACT.Copy).then_inc(a_w2, 1)

            def h_hi(n, t):
                t_hT.wait(act, n, t)
                act.activation(hT[n.u][HI][:, :, t * P:(t + 1) * P], bX[:, :].rearrange("p (k n) -> p k n", k=KT),
                               ACT.Copy).then_inc(a_hT.sem, 1)

            if first:
                t_proj.wait(act, static(NU - 1), UT - 1)
                for t in range(ST):
                    h_hi(s, t)
                split_hi(0)
                split_hi(1)
            for j in range(JT):
                t_fc1.wait(act, s, j)
                v_glo.wait(act, s, j - 1)
                act.activation(g[:, :], bF[j % 2][:, :], ACT.Gelu, bias=fc1_bias[:, j:j + 1]).then_inc(a_gelu.sem, 1)
                if first and j + 2 < JT:
                    split_hi(j + 2)
                if not last and j - 1 in NORMS:
                    h_hi(s.plus(1), NORMS.index(j - 1))

        blocks(act, step2)

    def vector_program(dve):
        for c in counts1:
            dve.sem_inc(c.sem, c.start)

        done = [0]

        def mark(ins):
            done[0] += 1
            ins.then_inc(v_set, 1)
            return done[0]

        def sync():
            dve.wait_ge(v_set, done[0])

        dve.wait_ge(d_ctx, 16)
        for b in range(B):
            i = dve.bn_stats(cbn[0:M, b, :], cx[0:M, b, :])
        mark(i)
        sync()
        for b in range(B):
            i = dve.bn_aggr(cmv[0:M, b, :], cbn[0:M, b, :])
        i.then_inc(s_chain, 1)
        dve.wait_ge(s_chain, 1)
        mark(dve.tensor_scalar(cve[0:M, :], cmv[0:M, :, 1], EPS, None, ALU.add))
        assert done[0] == 2
        dve.wait_ge(p_crs, 1)
        for b in range(B):
            i = dve.tensor_scalar(cx[0:M, b, :], cx[0:M, b, :], cmv[0:M, b, 0:1], crs[0:M, b:b + 1],
                                  ALU.subtract, ALU.mult)
        cx_norm = mark(i)
        dve.wait_ge(t_set, 1)
        cols_out = mark(dve.tensor_copy(cols[:, :], bank[0][:, 0:40]))
        assert (cx_norm, cols_out) == (3, 4)
        dve.wait_ge(d_qw, 16)
        sync()
        dve.tensor_scalar(wscale[:, :], cols[:, QNW:QNW + KT], SCALE, None, ALU.mult).then_inc(s_chain, 1)
        dve.wait_ge(s_chain, 2)
        dve.wait_ge(t_set, 2)
        for k in range(KT):
            i = dve.tensor_scalar(qraw[:, k, :], qraw[:, k, :], wscale[:, k:k + 1], None, ALU.mult)
        i.then_inc(s_chain, 1)
        dve.tensor_scalar(qbias[:, :], bank[1][:, 0:KT], SCALE, None, ALU.mult)
        dve.wait_ge(s_chain, 3)
        dve.tensor_copy(wq[HI][:, :, :], qraw[:, :, :]).then_inc(s_chain, 1)
        dve.wait_ge(s_chain, 4)
        wq_out = mark(dve.tensor_tensor(wq[LO][:, :, :], qraw[:, :, :], f32(wq[HI][:, :, :]), ALU.subtract))
        assert wq_out == 5

        def context():
            dve.wait_ge(t_set, 3)
            for b in range(B):
                for k in range(KT):
                    i = dve.tensor_scalar(cxT[:, k, b, :], bank[2 + b][:, k * M:(k + 1) * M],
                                          cols[:, CNW + k:CNW + k + 1], cols[:, CNB + k:CNB + k + 1], ALU.mult, ALU.add)
            assert mark(i) == 6
            dve.wait_ge(t_set, 4)
            dve.wait_ge(p_zero, 4)
            for part in (HI, LO):
                for b in range(B):
                    for h in range(HG):
                        r = slice(h * D, (h + 1) * D)
                        src = bank[4 + b][r, 0:GM].rearrange("p (g m) -> p g m", g=KT)
                        dst = kbd[part][r, b, :, h * M:(h + 1) * M]
                        if part == HI:
                            i = dve.tensor_copy(dst, src)
                        else:
                            i = dve.tensor_tensor(dst, src, f32(kbd[HI][r, b, :, h * M:(h + 1) * M]), ALU.subtract)
                if part == HI:
                    i.then_inc(s_chain, 1)
                    dve.wait_ge(s_chain, 5)
            assert mark(i) == 7
            dve.wait_ge(t_set, 5)
            for b in range(B):
                i = dve.tensor_copy(vtok[HI][0:M, b, :], bank[6 + b][0:M, :])
            i.then_inc(s_chain, 1)
            dve.wait_ge(s_chain, 6)
            for b in range(B):
                i = dve.tensor_tensor(vtok[LO][0:M, b, :], bank[6 + b][0:M, :], f32(vtok[HI][0:M, b, :]), ALU.subtract)
            assert mark(i) == 8

        def proj_weights():
            dve.wait_ge(d_pw, 16)
            dve.tensor_copy(wp[HI][:, :, :], praw[:, :, :]).then_inc(s_chain, 1)
            dve.wait_ge(s_chain, 7)
            assert mark(dve.tensor_tensor(wp[LO][:, :, :], praw[:, :, :], f32(wp[HI][:, :, :]), ALU.subtract)) == 9

        def step(k, back=False, scores=False, front=False, norm=False):
            b, s, f, n = k, k.plus(1), k.plus(2), k.plus(3)

            def masked(t, g_):
                i = t * KT + g_
                if i == 0:
                    p_neg.wait(dve, s, 0)
                    t_probT.wait(dve, s.plus(-2), KT * UT - 1)
                t_scores.wait(dve, s, i)
                dve.tensor_tensor(S[:, s.u, t, g_ * GM:(g_ + 1) * GM].rearrange("p (h m) -> p h m", h=HG),
                                  bS[i % 2][:, 0:GM].rearrange("p (h m) -> p h m", h=HG),
                                  negm[:, s.u, t, :].unsqueeze(1).to_broadcast([P, HG, M]),
                                  ALU.add).then_inc(v_scores.sem, 1)

            def maximum(t):
                v_scores.wait(dve, s, (t + 1) * KT - 1)
                dve.tensor_reduce(nmax[:, s.u, t, :], S[:, s.u, t, :].rearrange("p (h m) -> p h m", h=H), AX.X,
                                  ALU.max, negate=True).then_inc(v_max.sem, 1)

            def x_lo(t):
                a_xT.wait(dve, f, t)
                v = slice(t * P, (t + 1) * P)
                dve.tensor_tensor(xT[LO][:, :, v], bA[t][:, :].rearrange("p (k n) -> p k n", k=KT),
                                  f32(xT[HI][:, :, v]), ALU.subtract).then_inc(v_xT.sem, 1)

            def q_lo(h):
                a_q.wait(dve, f, h)
                for m in (2 * h, 2 * h + 1):
                    i = dve.scalar_tensor_tensor(out=qT[LO][:, m, :], in0=bA[h][:, (m % 2) * UN:(m % 2 + 1) * UN],
                                                 scalar=qbias[:, m:m + 1], in1=f32(qT[HI][:, m, :]),
                                                 op0=ALU.add, op1=ALU.subtract)
                i.then_inc(v_q.sem, 1)

            def prob_lo(g_):
                for t in range(UT):
                    i = g_ * UT + t
                    v = slice(t * P, (t + 1) * P)
                    a_probT.wait(dve, b, i)
                    dve.tensor_tensor(PT[LO][:, g_ % 2, :, v],
                                      bT[i % 2][:, 0:NC * P].rearrange("p (c n) -> p c n", c=NC),
                                      f32(PT[HI][:, g_ % 2, :, v]), ALU.subtract).then_inc(v_probT.sem, 1)

            def av_lo(g_):
                a_av.wait(dve, b, g_)
                dve.tensor_tensor(aT[LO][:, g_, :], bV[g_ % 2][:, 0:UN], f32(aT[HI][:, g_, :]),
                                  ALU.subtract).then_inc(v_av.sem, 1)

            def recip(t):
                a_exp.wait(dve, s, t)
                dve.reciprocal(rsum[:, s.u, t, :], esum[:, s.u, t, :]).then_inc(v_rsum.sem, 1)

            def stats():
                dve.wait_ge(d_x[n.u], n.q * 16 + 16)
                for t in range(UT):
                    dve.bn_stats(bnst[:, t, :], xr[:, bass.ds(n.slot(), 1), t, :]).then_inc(v_bn.sem, 1)

            def variance():
                for t in range(UT):
                    dve.bn_aggr(mv[:, t, :], bnst[:, t, :]).then_inc(v_mv.sem, 1)
                v_mv.wait(dve, n, UT - 1)
                dve.tensor_scalar(veps[:, :], mv[:, :, 1], EPS, None, ALU.add).then_inc(v_veps.sem, 1)

            def normed():
                p_rstd.wait(dve, n, 0)
                for t in range(UT):
                    t_xT.wait(dve, n.plus(-1), t)
                    dve.tensor_scalar(xhat[:, t:t + 1, :], xr[:, bass.ds(n.slot(), 1), t, :], mv[:, t, 0:1],
                                      rstd[:, t:t + 1], ALU.subtract, ALU.mult).then_inc(v_xhat.sem, 1)

            def residual(t):
                t_proj.wait(dve, b, t)
                p_projb.wait(dve, b, t)
                v = xr[:, bass.ds(b.slot(), 1), t, :]
                dve.tensor_tensor(v, bV[t][:, :].unsqueeze(1), v, ALU.add).then_inc(v_res.sem, 1)

            if scores:
                for g_ in range(KT):
                    masked(0, g_)
            if front:
                x_lo(0)
                x_lo(1)
            if scores:
                masked(1, 0)
                masked(1, 1)
                maximum(0)
            if back:
                prob_lo(0)
            if scores:
                masked(1, 2)
                masked(1, 3)
                maximum(1)
            if back:
                prob_lo(1)
                av_lo(0)
            if front:
                q_lo(0)
            if back:
                prob_lo(2)
                av_lo(1)
                prob_lo(3)
            if norm:
                stats()
                v_bn.wait(dve, n, UT - 1)
            if scores:
                recip(0)
            if norm:
                variance()
            if back:
                av_lo(2)
            if front:
                q_lo(1)
            if back:
                av_lo(3)
            if norm:
                normed()
            if back:
                residual(0)
            if scores:
                recip(1)
            if back:
                residual(1)
            if isinstance(k.q, int) and k.q == -1 and k.u == 0:
                context()
                proj_weights()

        pipeline(dve, step)

        def step2(s, first=False, last=False):
            def split_lo(j):
                dve.wait_ge(t_bias, j + 1)
                dve.tensor_tensor(fc1_bias[:, j:j + 1], bB[:, j:j + 1], cols[:, F1B + j:F1B + j + 1],
                                  ALU.add).then_inc(v_bias, 1)
                dve.wait_ge(a_w1, j + 1)
                dve.tensor_tensor(w1[:, j, LO, :, :], w1raw[:, j % 2, :, :], f32(w1[:, j, HI, :, :]),
                                  ALU.subtract).then_inc(v_w1, 1)
                dve.wait_ge(a_w2, j + 1)
                dve.tensor_tensor(w2[:, j, LO, :], w2raw[:, :], f32(w2[:, j, HI, :]),
                                  ALU.subtract).then_inc(v_w2, 1)

            def stats(n, t):
                if t == 0:
                    dve.wait_ge(d_x2[n.u], n.q * 16 + 16)
                dve.bn_stats(hbn[:, :], x2[n.u][:, t, :]).then_inc(v_hbn.sem, 1)

            def variance(n, t):
                dve.bn_aggr(hmv[:, :], hbn[:, :]).then_inc(v_hmv.sem, 1)
                v_hmv.wait(dve, n, t)
                dve.tensor_scalar(hve[:, :], hmv[:, 1:2], EPS, None, ALU.add).then_inc(v_hve.sem, 1)

            def normed(n, t):
                p_hrs.wait(dve, n, t)
                t_hT.wait(dve, n, t - 1)
                dve.tensor_scalar(hhat[:, :], x2[n.u][:, t, :], hmv[:, 0:1], hrs[:, 0:1], ALU.subtract,
                                  ALU.mult).then_inc(v_hhat.sem, 1)

            def h_lo(n, t):
                a_hT.wait(dve, n, t)
                v = slice(t * P, (t + 1) * P)
                dve.tensor_tensor(hT[n.u][LO][:, :, v], bX[:, :].rearrange("p (k n) -> p k n", k=KT),
                                  f32(hT[n.u][HI][:, :, v]), ALU.subtract).then_inc(v_hT.sem, 1)

            def output(n, t):
                t_fc2.wait(dve, n, (JT - 1) * ST + t)
                p_fc2b.wait(dve, n, t)
                dve.tensor_tensor(x2[n.u][:, t, :], bC[t][:, :], x2[n.u][:, t, :], ALU.add).then_inc(v_out.sem, 1)

            if first:
                for t in range(ST):
                    stats(s, t)
                    v_hbn.wait(dve, s, t)
                    variance(s, t)
                    normed(s, t)
                    if t:
                        h_lo(s, t - 1)
                h_lo(s, ST - 1)
                split_lo(0)
                split_lo(1)
            for j in range(JT):
                a_gelu.wait(dve, s, j)
                t_fc2.wait(dve, s, (j - 3) * ST - 1)
                dve.tensor_copy(gT[HI][:, j % 4, :], g[:, :]).then_inc(v_ghi.sem, 1)
                norming = not last and j in NORMS
                if norming:
                    stats(s.plus(1), NORMS.index(j))
                    v_hbn.wait(dve, s.plus(1), NORMS.index(j))
                v_ghi.wait(dve, s, j)
                dve.tensor_tensor(gT[LO][:, j % 4, :], g[:, :], f32(gT[HI][:, j % 4, :]),
                                  ALU.subtract).then_inc(v_glo.sem, 1)
                if first and j + 2 < JT:
                    split_lo(j + 2)
                if not first and j == 1:
                    for t in range(ST):
                        output(s.plus(-1), t)
                if not last and j - 2 in NORMS:
                    h_lo(s.plus(1), NORMS.index(j - 2))
                if norming:
                    variance(s.plus(1), NORMS.index(j))
                    normed(s.plus(1), NORMS.index(j))
            if last:
                for t in range(ST):
                    output(s, t)

        blocks(dve, step2)

    def tensor_program(pe):
        pe.wait_ge(d_rows, 16 * 7)
        pe.wait_ge(p_ident, 2)
        pe.transpose(bank[0][:, 0:40], rows[:, :], ident[0:40, 0:40]).then_inc(t_set, 1)
        pe.wait_ge(v_set, 4)
        pe.wait_ge(d_qw, 16)
        for m in range(KT):
            for k in range(KT):
                i = pe.matmul(bank[1][:, m:m + 1], qraw[:, k, m * P:(m + 1) * P], cols[:, QNB + k:QNB + k + 1],
                              start=(k == 0), stop=(k == KT - 1))
        i.then_inc(t_set, 1)
        for b in range(B):
            for k in range(KT):
                i = pe.transpose(bank[2 + b][:, k * M:(k + 1) * M], cx[0:M, b, k * P:(k + 1) * P], ident[0:M, 0:M])
        i.then_inc(t_set, 1)

        def context():
            pe.wait_ge(v_set, 6)
            pe.wait_ge(d_kvw, 16)
            for b in range(B):
                for g_ in range(KT):
                    for k in range(KT):
                        i = pe.matmul(bank[4 + b][:, g_ * M:(g_ + 1) * M], kvw[:, k, g_ * P:(g_ + 1) * P],
                                      cxT[:, k, b, :], start=(k == 0), stop=(k == KT - 1))
            i.then_inc(t_set, 1)
            for b in range(B):
                for k in range(KT):
                    i = pe.matmul(bank[6 + b][0:M, :], cxT[:, k, b, :], kvw[:, k, C:2 * C],
                                  start=(k == 0), stop=(k == KT - 1))
            i.then_inc(t_set, 1)
            pe.wait_ge(v_set, 7)

        def step(k, back=False, scores=False, front=False, norm=False):
            b, s, f = k, k.plus(1), k.plus(2)

            def score(t, g_):
                i = t * KT + g_
                if i == 0:
                    v_q.wait(pe, s, UT - 1)
                v_scores.wait(pe, s, i - 2)
                for n, (w, d) in enumerate(PRODUCTS):
                    mm = pe.matmul(bS[i % 2][:, 0:GM], qT[d][:, g_, t * P:(t + 1) * P], kbd[w][:, s.u, g_, :],
                                   start=(n == 0), stop=(n == 2))
                mm.then_inc(t_scores.sem, 1)

            def x_T(t):
                v_xhat.wait(pe, f, t)
                v_q.wait(pe, f.plus(-1), t)
                for c in range(KT):
                    mm = pe.transpose(bA[t][:, c * P:(c + 1) * P], xhat[:, t, c * P:(c + 1) * P], ident[:, :])
                mm.then_inc(t_xT.sem, 1)

            def q(m):
                if m == 0:
                    v_xT.wait(pe, f, UT - 1)
                n = 0
                for c in range(KT):
                    for w, d in PRODUCTS:
                        mm = pe.matmul(bA[m // 2][:, (m % 2) * UN:(m % 2 + 1) * UN], wq[w][:, c, m * P:(m + 1) * P],
                                       xT[d][:, c, :], start=(n == 0), stop=(n == 3 * KT - 1))
                        n += 1
                if m % 2:
                    mm.then_inc(t_q.sem, 1)

            def prob_T(g_):
                for t in range(UT):
                    i = g_ * UT + t
                    if g_ == 0:
                        p_prob.wait(pe, b, t)
                    v_probT.wait(pe, b, i - 2)
                    for c in range(NC):
                        r = g_ * GM + CH0[c]
                        mm = pe.transpose(bT[i % 2][:, c * P:(c + 1) * P], S[:, b.u, t, r:r + P], ident[:, :])
                    mm.then_inc(t_probT.sem, 1)

            def av(g_):
                v_probT.wait(pe, b, g_ * UT + UT - 1)
                if g_ < 2:
                    v_res.wait(pe, b.plus(-1), g_)
                else:
                    v_av.wait(pe, b, g_ - 2)
                n = 0
                for c in range(NC):
                    for w, d in PRODUCTS:
                        mm = pe.matmul(bV[g_ % 2][:, 0:UN], vbd[w][:, b.u, g_ * NC + c, :], PT[d][:, g_ % 2, c, :],
                                       start=(n == 0), stop=(n == 3 * NC - 1))
                        n += 1
                mm.then_inc(t_av.sem, 1)

            def proj(t):
                n = 0
                for c in range(KT):
                    if t == 0 and c in (0, KT - 1):
                        v_av.wait(pe, b, KT - 2 + (c > 0))
                    for w, d in PRODUCTS:
                        mm = pe.matmul(bV[t][:, :], aT[d][:, c, t * P:(t + 1) * P], wp[w][:, c, :],
                                       start=(n == 0), stop=(n == 3 * KT - 1))
                        n += 1
                mm.then_inc(t_proj.sem, 1)

            if scores:
                for g_ in range(KT):
                    score(0, g_)
            if front:
                x_T(0)
                x_T(1)
            if scores:
                score(1, 0)
                score(1, 1)
            if back:
                prob_T(0)
            if front:
                q(0)
            if scores:
                score(1, 2)
                score(1, 3)
            if back:
                prob_T(1)
            if front:
                q(1)
            if back:
                av(0)
                prob_T(2)
            if front:
                q(2)
            if back:
                av(1)
                prob_T(3)
            if front:
                q(3)
            if back:
                av(2)
                av(3)
                proj(0)
                proj(1)
            if isinstance(k.q, int) and k.q == -1 and k.u == 0:
                context()
            if isinstance(k.q, int) and k.q == -1 and k.u == 1:
                pe.wait_ge(d_vbd, 16 * 24)
                pe.wait_ge(v_set, 9)

        pe.wait_ge(v_set, 5)
        pipeline(pe, step)

        def step2(s, first=False, last=False):
            def bias(j):
                pe.wait_ge(d_w1[j % 2], 16 * (j // 2) + 16)
                if j:
                    pe.wait_ge(v_bias, j)
                for k in range(KT):
                    mm = pe.matmul(bB[:, j:j + 1], w1raw[:, j % 2, k, :], cols[:, N2B + k:N2B + k + 1],
                                   start=(k == 0), stop=(k == KT - 1))
                mm.then_inc(t_bias, 1)

            def h_T(n, t):
                v_hhat.wait(pe, n, t)
                v_hT.wait(pe, n, t - 1)
                for c in range(KT):
                    mm = pe.transpose(bX[:, c * P:(c + 1) * P], hhat[:, c * P:(c + 1) * P], ident[:, :])
                mm.then_inc(t_hT.sem, 1)

            def fc1(j):
                if first:
                    pe.wait_ge(v_w1, j + 1)
                if j == 0:
                    v_hT.wait(pe, s, ST - 1)
                a_gelu.wait(pe, s, j - 2)
                n = 0
                for c in range(KT):
                    for w, d in PRODUCTS:
                        mm = pe.matmul(bF[j % 2][:, :], w1[:, j, w, c, :], hT[s.u][d][:, c, :],
                                       start=(n == 0), stop=(n == 3 * KT - 1))
                        n += 1
                mm.then_inc(t_fc1.sem, 1)

            def fc2(n, j):
                if first:
                    pe.wait_ge(v_w2, j + 1)
                v_glo.wait(pe, n, j)
                for t in range(ST):
                    if j == 0:
                        v_out.wait(pe, n.plus(-1), t)
                    for i, (w, d) in enumerate(PRODUCTS):
                        mm = pe.matmul(bC[t][:, :], gT[d][:, j % 4, t * P:(t + 1) * P], w2[:, j, w, :],
                                       start=(j == 0 and i == 0), stop=(j == JT - 1 and i == 2))
                    mm.then_inc(t_fc2.sem, 1)

            if first:
                v_res.wait(pe, static(NU - 1), UT - 1)
                for t in range(ST):
                    h_T(s, t)
                bias(0)
                bias(1)
            for j in range(JT):
                fc1(j)
                if first and j + 2 < JT:
                    bias(j + 2)
                if j >= 2:
                    fc2(s, j - 2)
                elif not first:
                    fc2(s.plus(-1), JT - 2 + j)
                if not last and j - 1 in NORMS:
                    h_T(s.plus(1), NORMS.index(j - 1))
            if first:
                pe.wait_ge(v_w2, JT)
            if last:
                fc2(s, JT - 2)
                fc2(s, JT - 1)

        blocks(pe, step2)

    with nc.Block() as block:
        block.sync(sync_program)
        block.gpsimd(gpsimd_program)
        block.scalar(scalar_program)
        block.vector(vector_program)
        block.tensor(tensor_program)


INPUTS = ["x", "ctx_1024", "mask_BxSxS2_bk0"] + [
    f"L0_xattn_{n}" for n in ("qn_w", "qn_b", "cn_w", "cn_b", "n2_w", "n2_b", "q_w", "kv_w", "proj_w", "proj_b",
                              "fc1_w", "fc1_b", "fc2_w", "fc2_b")]


def kernel(**inputs):
    import numpy as np
    import concourse.bacc as bacc
    from concourse.bass_utils import run_bass_kernel_spmd

    nc = bacc.Bacc("TRN2", target_bir_lowering=False, num_devices=1)
    arrays, args = {}, []
    for name in INPUTS:
        a = np.ascontiguousarray(inputs[name])
        arrays[f"in_{name}"] = a
        args.append(nc.dram_tensor(f"in_{name}", a.shape, mybir.dt.from_np(a.dtype), kind="ExternalInput").ap())
    args.append(nc.dram_tensor("out_0", inputs["x"].shape, F32, kind="ExternalOutput").ap())
    build_block(nc, *args)
    return run_bass_kernel_spmd(nc, [arrays], core_ids=[0]).results[0]["out_0"]
```

```python
import concourse.bass as bass
from concourse import mybir

F32 = mybir.dt.float32
F32R = mybir.dt.float32r
U8 = mybir.dt.uint8
ALU = mybir.AluOpType
ACT = mybir.ActivationFunctionType
AX = mybir.AxisListType

P = 128
EPS = 1e-5
FLT_MAX = 3.4028234663852886e38
HI, LO = 0, 1
PRODUCTS = ((HI, HI), (LO, HI), (HI, LO))


class Unit:

    def __init__(self, q, u):
        self.q, self.u = q, u

    def plus(self, d):
        return Unit(self.q + (self.u + d) // 2, (self.u + d) % 2)

    def slot(self):
        return (self.q % 2) * 2 + self.u


class Count:

    def __init__(self, nc, name, per, start=0):
        self.sem, self.per, self.start = nc.alloc_semaphore(name), per, start

    def after(self, unit, i):
        return unit.q * (2 * self.per) + (unit.u * self.per + self.start + i + 1)

    def wait(self, eng, unit, i):
        value = self.after(unit, i)
        if isinstance(value, int) and value <= self.start:
            return
        eng.wait_ge(self.sem, value)


def build_block(nc, x, ctx, mask, qn_w, qn_b, cn_w, cn_b, n2_w, n2_b, q_w, kv_w, proj_w, proj_b,
                fc1_w, fc1_b, fc2_w, fc2_b, out):
    B, N, C = x.shape
    M = ctx.shape[1]
    HID = fc1_w.shape[1]
    H = 16
    D = C // H
    SCALE = D ** -0.5
    KT = C // P
    HG = P // D
    GM = HG * M
    UT = 2
    UN = UT * P
    NU = B * N // UN
    NC = -(-GM // P)
    CH0 = [c * (GM - P) // (NC - 1) for c in range(NC)]
    CH0[-1] = GM - P
    SB = 512
    ST = SB // P
    NS = B * N // SB
    JT = HID // P
    assert B == 2 and N % UN == 0 and NU % 2 == 0 and NU >= 8 and NS % 2 == 0 and NS >= 4

    x_v = x.rearrange("b (n t p) c -> b p n t c", t=UT, p=P)
    mask_v = mask.rearrange("b (n t p) m -> b p n t m", t=UT, p=P)
    x2_dram = nc.dram_tensor("x2_scratch", [B * N, C], F32, kind="Internal").ap()
    x2_units = x2_dram.rearrange("(b n t p) c -> b p n t c", b=B, t=UT, p=P)
    x2_blocks = x2_dram.rearrange("(s t p) c -> p s t c", t=ST, p=P)
    out_blocks = out.rearrange("b n c -> (b n) c").rearrange("(s t p) c -> p s t c", t=ST, p=P)
    fc1_v = fc1_w.rearrange("(k p) (j n) -> j p k n", p=P, n=P)
    fc2_v = fc2_w.rearrange("(j p) n -> j p n", p=P)

    base = 16512
    top = [base]

    def at(name, shape, dt, offset=None):
        size = 1 if dt is U8 else 4
        for s in shape[1:]:
            size *= s
        if offset is None:
            offset = top[0]
            top[0] += (size + 31) // 32 * 32
        return nc.alloc_sbuf_tensor_at(name, shape, dt, offset=offset)

    ident = at("ident", [P, P], F32)
    cols = at("cols", [P, 40], F32)
    fc1_bias = at("fc1_bias", [P, JT], F32)
    qbias = at("qbias", [P, KT], F32)
    mhalf = at("mhalf", [P, 4], F32)
    wscale = at("wscale", [P, KT], F32)
    region1 = top[0]

    wq = [at(f"wq{s}", [P, KT, C], F32R) for s in "hl"]
    kbd = [at(f"kbd{s}", [P, B, KT, GM], F32R) for s in "hl"]
    xT = [at(f"xT{s}", [P, KT, UN], F32R) for s in "hl"]
    qT = [at(f"qT{s}", [P, KT, UN], F32R) for s in "hl"]
    xhat = at("xhat", [P, UT, C], F32)
    wp = [at(f"wp{s}", [P, KT, C], F32R) for s in "hl"]
    vbd = [at(f"vbd{s}", [P, B, KT * NC, P], F32R) for s in "hl"]
    S = at("S", [P, 2, UT, H * M], F32)
    PT = [at(f"PT{s}", [P, 2, NC, UN], F32R) for s in "hl"]
    aT = [at(f"aT{s}", [P, KT, UN], F32R) for s in "hl"]
    xr = at("xr", [P, 4, UT, C], F32)
    projb = at("projb", [P, C], F32)
    mask_in = at("mask_in", [P, 2, UT, M], U8)
    negm = at("negm", [P, 2, UT, M], F32)
    bnst = at("bnst", [P, UT, 6], F32)
    mv = at("mv", [P, UT, 2], F32)
    veps = at("veps", [P, UT], F32)
    rstd = at("rstd", [P, UT], F32)
    region2 = top[0]

    kvw = at("kvw", [P, KT, 2 * C], F32)
    qraw = at("qraw", [P, KT, C], F32)
    praw = at("praw", [P, KT, C], F32)
    cx = at("cx", [P, B, C], F32)
    cxT = at("cxT", [P, KT, B, M], F32)
    vtok = [at(f"vtok{s}", [P, B, C], F32R) for s in "hl"]
    rows = at("rows", [40, P], F32)
    cbn = at("cbn", [P, B, 6], F32)
    cmv = at("cmv", [P, B, 2], F32)
    cve = at("cve", [P, B], F32)
    crs = at("crs", [P, B], F32)
    end0 = top[0]

    top[0] = region2
    x2_0 = at("x2_0", [P, ST, C], F32)
    hT_0 = [at(f"hT0{s}", [P, KT, SB], F32R) for s in "hl"]
    w1raw = at("w1raw", [P, 2, KT, P], F32)
    w2raw = at("w2raw", [P, 2, C], F32)
    hhat = at("hhat", [P, C], F32)
    fc2b = at("fc2b", [P, C], F32)
    gT_start = top[0]
    gT = [at(f"gT{s}", [P, 4, SB], F32R) for s in "hl"]
    gT_end = top[0]
    hbn = at("hbn", [P, 6], F32)
    hmv = at("hmv", [P, 2], F32)
    hve = at("hve", [P, 1], F32)
    hrs = at("hrs", [P, 1], F32)
    end2 = top[0]
    top[0] = max(end0, gT_start)
    nmax = at("nmax", [P, 2, UT, H], F32)
    esum = at("esum", [P, 2, UT, H], F32)
    rsum = at("rsum", [P, 2, UT, H], F32)
    assert top[0] <= gT_end, (top[0], gT_start, gT_end, end0)
    top[0] = region1
    w1 = at("w1", [P, JT, 2, KT, P], F32R)
    w2 = at("w2", [P, JT, 2, C], F32R)
    x2_1 = at("x2_1", [P, ST, C], F32)
    hT_1 = [at(f"hT1{s}", [P, KT, SB], F32R) for s in "hl"]
    g = at("g", [P, SB], F32)
    assert top[0] <= region2 and max(end0, end2) <= 229344, (top[0], region2, end0, end2)
    x2 = [x2_0, x2_1]
    hT = [hT_0, hT_1]

    QNW, QNB, CNW, CNB, N2W, N2B, F1B = (4 * i for i in range(7))

    bank = [nc.alloc_psum_tensor(f"bank{i}", [P, 512], F32) for i in range(8)]
    bA, bS, bT, bV = bank[0:2], bank[2:4], bank[4:6], bank[6:8]
    bC, bF, bX, bB = [bank[i] for i in (0, 1, 6, 7)], bank[2:4], bank[4], bank[5]

    def sem(name):
        return nc.alloc_semaphore(name)

    d_rows, d_ctx, d_kw, d_vw, d_qw, d_pw, d_projb = (sem(f"d_{n}") for n in
                                                      ("rows", "ctx", "kw", "vw", "qw", "pw", "projb"))
    d_vbd = [sem("d_vbd0"), sem("d_vbd1")]
    d_x = [sem("d_x0"), sem("d_x1")]
    d_mask = [sem("d_mask0"), sem("d_mask1")]
    d_x2st = sem("d_x2st")
    p_ident, p_half, p_zero, p_crs = (sem(f"p_{n}") for n in ("ident", "half", "zero", "crs"))
    t_cols, v_cols, v_cve, v_ctx, t_ctxT, v_ctxT = (sem(n) for n in
                                                    ("t_cols", "v_cols", "v_cve", "v_ctx", "t_ctxT", "v_ctxT"))
    t_keys, a_keys, v_keys, t_vals, a_vals, v_vals = (sem(n) for n in
                                                      ("t_keys", "a_keys", "v_keys", "t_vals", "a_vals", "v_vals"))
    t_qbias, v_qbias, v_wscale, a_wq, v_wq, a_wp, v_wp = (sem(n) for n in ("t_qbias", "v_qbias", "v_wscale", "a_wq",
                                                                           "v_wq", "a_wp", "v_wp"))

    def count(name, per, start=0):
        return Count(nc, name, per, start)

    t_scores = count("t_scores", UT * KT)
    v_scores = count("v_scores", UT * KT, 2)
    v_max = count("v_max", UT)
    a_exp = count("a_exp", UT)
    v_rsum = count("v_rsum", UT)
    p_prob = count("p_prob", UT)
    t_probT = count("t_probT", KT * UT, 1)
    a_probT = count("a_probT", KT * UT)
    v_probT = count("v_probT", KT * UT, 2)
    t_av = count("t_av", KT, 2)
    a_av = count("a_av", KT)
    v_av = count("v_av", KT)
    t_proj = count("t_proj", UT, 1)
    v_res = count("v_res", UT, 2)
    t_xT = count("t_xT", UT)
    a_xT = count("a_xT", UT)
    v_xT = count("v_xT", UT)
    t_q = count("t_q", UT, 1)
    a_q = count("a_q", UT)
    v_q = count("v_q", UT, 2)
    v_bn, v_mv, v_veps = count("v_bn", UT), count("v_mv", UT), count("v_veps", 1)
    p_rstd = count("p_rstd", 1)
    v_xhat = count("v_xhat", UT)
    p_projb = count("p_projb", UT)
    p_neg = count("p_neg", 1)
    counts1 = [v_scores, t_probT, v_probT, t_av, t_proj, v_res, t_q, v_q]

    d_w1 = [sem("d_w1_0"), sem("d_w1_1")]
    d_w2 = [sem("d_w2_0"), sem("d_w2_1")]
    d_fc2b, d_out = sem("d_fc2b"), sem("d_out")
    d_x2 = [sem("d_x2_0"), sem("d_x2_1")]
    t_bias, v_bias, a_w1, v_w1, a_w2, v_w2 = (sem(n) for n in ("t_bias", "v_bias", "a_w1", "v_w1", "a_w2", "v_w2"))
    v_hbn, v_hmv, v_hve = count("v_hbn", ST), count("v_hmv", ST), count("v_hve", ST)
    p_hrs, v_hhat = count("p_hrs", ST), count("v_hhat", ST)
    t_hT, a_hT, v_hT = count("t_hT", ST), count("a_hT", ST), count("v_hT", ST)
    t_fc1 = count("t_fc1", JT)
    a_gelu = count("a_gelu", JT)
    v_ghi = count("v_ghi", JT)
    v_glo = count("v_glo", JT)
    t_fc2 = count("t_fc2", JT * ST)
    v_out = count("v_out", ST)
    p_fc2b = count("p_fc2b", ST)

    def f32(ap):
        return ap.bitcast(F32)

    def units(lo, hi, eng, body):
        with eng.Fori(lo // 2, hi // 2) as q:
            for u in range(2):
                body(Unit(q, u))

    def static(n):
        return Unit(n // 2, n % 2)

    LOOP = (0, (NU - 4) // 2 * 2)

    def pipeline(eng, step):
        step(static(-3), norm=True)
        step(static(-2), front=True, norm=True, keys_too=True)
        step(static(-1), scores=True, front=True, norm=True, values_too=True)
        units(*LOOP, eng, lambda k: step(k, back=True, scores=True, front=True, norm=True))
        for n in range(LOOP[1], NU):
            step(static(n), back=True, scores=n + 1 < NU, front=n + 2 < NU, norm=n + 3 < NU, tail=n == NU - 1)

    NORMS = [5 + 2 * t for t in range(ST)]
    assert NORMS[-1] + 2 < JT

    def blocks(eng, step):
        step(static(0), first=True)
        with eng.Fori(0, (NS - 2) // 2) as i:
            step(Unit(i, 1))
            step(Unit(i + 1, 0))
        step(static(NS - 1), last=True)

    last_unit = static(NU - 1)
    s_chain = sem("v_chain")
    v_zero = sem("v_zero")
    p_less = count("p_less", 1)
    v_esum = count("v_esum", 1)

    def bias_bank(j):
        return bF[j] if j < 2 else bB

    def h_bank(n, t):
        return bank[t % 2] if isinstance(n.q, int) and n.q == 0 and n.u == 0 else bX

    def sync_program(sp):
        def load_x(n):
            sp.dma_start(xr[:, bass.ds(n.slot(), 1), :, :],
                         x_v[n.u][:, bass.ds(n.q, 1), :, :]).then_inc(d_x[n.u], 16)

        def load_mask(n):
            sp.dma_start(mask_in[:, n.u:n.u + 1, :, :],
                         mask_v[n.u][:, bass.ds(n.q, 1), :, :]).then_inc(d_mask[n.u], 16)

        load_x(static(0))
        for i, v in enumerate((qn_w, qn_b, cn_w, cn_b, n2_w, n2_b)):
            sp.dma_start(rows[4 * i:4 * i + 4, :], v.rearrange("(k p) -> k p", p=P)).then_inc(d_rows, 16)
        sp.dma_start(rows[24:40, :], fc1_b.rearrange("(k p) -> k p", p=P)).then_inc(d_rows, 16)
        load_x(static(1))
        load_mask(static(0))
        load_mask(static(1))
        sp.dma_start(projb[:, :], proj_b.rearrange("(a c) -> a c", a=1).to_broadcast([P, C])).then_inc(d_projb, 16)
        for n in (2, 3):
            sp.wait_ge(d_x[n % 2], 16)
            load_x(static(n))
        sp.wait_ge(v_vals, 1)
        sp.wait_ge(p_zero, 2)
        for part, b, h, c in ((part, b, h, c) for b in range(B) for part in (HI, LO) for h in range(HG) for c in range(NC)):
            own = 0 if c == 0 else CH0[c - 1] + P
            r0, r1 = max(h * M, own), min((h + 1) * M, CH0[c] + P)
            if r0 < r1:
                sp.dma_start(
                    f32(vbd[part][r0 - CH0[c]:r1 - CH0[c], b, :, :]).rearrange("p (g c) n -> p g c n", c=NC)[
                        :, :, c, h * D:(h + 1) * D],
                    f32(vtok[part][r0 - h * M:r1 - h * M, b, :]).rearrange("p (g n) -> p g n", g=KT)[
                        :, :, h * D:(h + 1) * D]).then_inc(d_vbd[b], 16)
        for n in (2, 3):
            p_neg.wait(sp, static(n - 2), 0)
            load_mask(static(n))

        def step(k, more=True):
            v_res.wait(sp, k, UT - 1)
            sp.dma_start(x2_units[k.u][:, bass.ds(k.q, 1), :, :],
                         xr[:, bass.ds(k.slot(), 1), :, :]).then_inc(d_x2st, 16)
            if more:
                sp.wait_ge(d_x2st, k.q * 32 + (k.u * 16 + 16))
                load_x(k.plus(4))
                load_mask(k.plus(4))

        units(0, NU - 4, sp, step)
        def load_w(j, which):
            b = j % 2
            if which == 1:
                if j >= 2:
                    sp.wait_ge(v_w1, j - 1)
                sp.dma_start(w1raw[:, b, :, :], fc1_v[j]).then_inc(d_w1[b], 16)
            else:
                if j >= 2:
                    sp.wait_ge(v_w2, j - 1)
                sp.dma_start(w2raw[:, b, :], fc2_v[j]).then_inc(d_w2[b], 16)

        def load_x2(s):
            sp.dma_start(x2[s.u][:, :, :].unsqueeze(1),
                         x2_blocks[:, bass.ds(s.q * 2 + s.u, 1), :, :]).then_inc(d_x2[s.u], 16)

        def store_out(s):
            v_out.wait(sp, s, ST - 1)
            sp.dma_start(out_blocks[:, bass.ds(s.q * 2 + s.u, 1), :, :],
                         x2[s.u][:, :, :].unsqueeze(1)).then_inc(d_out, 16)
            sp.wait_ge(d_out, s.q * 32 + (s.u * 16 + 16))

        step(static(NU - 4), more=False)
        load_x2(static(0))
        sp.dma_start(fc2b[:, :], fc2_b.rearrange("(a c) -> a c", a=1).to_broadcast([P, C])).then_inc(d_fc2b, 16)
        for j in range(2):
            load_w(j, 1)
            load_w(j, 2)
        for n in range(NU - 3, NU):
            step(static(n), more=False)
        t_proj.wait(sp, last_unit, UT - 1)
        sp.wait_ge(d_x2st, 16 * NU)
        load_w(2, 1)
        load_w(2, 2)
        load_x2(static(1))
        for j in range(3, JT):
            load_w(j, 1)
            load_w(j, 2)
        store_out(static(0))
        load_x2(static(2))
        with sp.Fori(0, (NS - 2) // 2 - 1) as i:
            for s in (Unit(i, 1), Unit(i + 1, 0)):
                store_out(s)
                load_x2(s.plus(2))
        store_out(static(NS - 3))
        load_x2(static(NS - 1))
        store_out(static(NS - 2))
        for t in range(ST):
            v_out.wait(sp, static(NS - 1), t)
            sp.dma_start(out_blocks[:, NS - 1, t, :], x2[(NS - 1) % 2][:, t, :]).then_inc(d_out, 16)
        sp.wait_ge(d_out, 16 * (NS - 1 + ST))

    def gpsimd_program(pool):
        pool.memset(mhalf[:, :], -0.5).then_inc(p_half, 1)
        pool.memset(ident[:, :], 0.0).then_inc(p_ident, 1)
        pool.wait_ge(p_ident, 1)
        pool.affine_select(out=ident[:, :], in_=ident[:, :], compare_op=ALU.not_equal, fill=1.0, base=0,
                           pattern=[[-1, P]], channel_multiplier=1).then_inc(p_ident, 1)
        pool.wait_ge(p_half, 1)

        def power(dst, src, n):
            return pool.tensor_tensor(dst, src, mhalf[0:n, 0:src.shape[1]], ALU.pow)

        pool.wait_ge(v_cve, 1)
        power(crs[0:M, :], cve[0:M, :], M).then_inc(p_crs, 1)

        def may_negate(n):
            pool.wait_ge(d_mask[n.u], n.q * 16 + 16)
            v_scores.wait(pool, n.plus(-2), UT * KT - 1)

        def negative(n):
            pool.tensor_scalar(negm[:, n.u, :, :], mask_in[:, n.u, :, :], -FLT_MAX, 1.0, ALU.mult,
                               ALU.mult).then_inc(p_neg.sem, 1)

        def step(k, back=False, scores=False, front=False, norm=False, keys_too=False, values_too=False, tail=False):
            def add_projb(t):
                v = xr[:, bass.ds(k.slot(), 1), t, :]
                pool.tensor_tensor(v, v, projb[:, :].unsqueeze(1), ALU.add).then_inc(p_projb.sem, 1)

            if front:
                may_negate(k.plus(2))
            if back:
                add_projb(0)
            if front:
                negative(k.plus(2))
            if back:
                add_projb(1)
            if scores:
                n = k.plus(1)
                v_max.wait(pool, n, 1)
                v = S[:, n.u, 1, :].rearrange("p (h m) -> p h m", h=H)
                pool.tensor_tensor(v, v, nmax[:, n.u, 1, :].unsqueeze(2).to_broadcast([P, H, M]),
                                   ALU.add).then_inc(p_less.sem, 1)
            if norm:
                n = k.plus(3)
                v_veps.wait(pool, n, 0)
                v_xhat.wait(pool, n.plus(-1), UT - 1)
                power(rstd[:, :], veps[:, :], P).then_inc(p_rstd.sem, 1)
                if isinstance(k.q, int) and k.q == -2:
                    for t in vbd:
                        pool.memset(f32(t[:, :, :, :]).rearrange("p a b c -> p (a b c)"), 0.0).then_inc(p_zero, 1)
                    pool.wait_ge(d_projb, 16)
            if scores:
                n = k.plus(1)
                for i, t in enumerate((1, 0)):
                    v_rsum.wait(pool, n, i)
                    v = S[:, n.u, t, :].rearrange("p (h m) -> p h m", h=H)
                    pool.tensor_tensor(v, v, rsum[:, n.u, t, :].unsqueeze(2).to_broadcast([P, H, M]),
                                       ALU.mult).then_inc(p_prob.sem, 1)

        pipeline(pool, step)

        def step2(s, first=False, last=False):
            def norm(n, t):
                v_hve.wait(pool, n, t)
                power(hrs[:, :], hve[:, :], P).then_inc(p_hrs.sem, 1)

            def bias(n, t):
                v_hhat.wait(pool, n, t)
                v = x2[n.u][:, t, :]
                pool.tensor_tensor(v, v, fc2b[:, :], ALU.add).then_inc(p_fc2b.sem, 1)

            if first:
                pool.wait_ge(d_fc2b, 16)
                for t in range(ST):
                    norm(s, t)
                    bias(s, t)
            for j in range(JT):
                if not last and j in NORMS:
                    norm(s.plus(1), NORMS.index(j))
                    bias(s.plus(1), NORMS.index(j))

        blocks(pool, step2)

    def scalar_program(act):
        act.dma_start(cx[0:M, :, :], ctx.rearrange("b m c -> m b c")).then_inc(d_ctx, 16)
        act.dma_start(qraw[:, :, :], q_w.rearrange("(k p) n -> p k n", p=P)).then_inc(d_qw, 16)
        act.dma_start(kvw[:, :, 0:C], kv_w[:, 0:C].rearrange("(k p) n -> p k n", p=P)).then_inc(d_kw, 16)
        act.dma_start(kvw[:, :, C:2 * C], kv_w[:, C:2 * C].rearrange("(k p) n -> p k n", p=P)).then_inc(d_vw, 16)
        act.dma_start(praw[:, :, :], proj_w.rearrange("(k p) n -> p k n", p=P)).then_inc(d_pw, 16)
        act.wait_ge(v_wscale, 1)
        act.wait_ge(d_qw, 16)
        for k in range(KT):
            act.activation(wq[HI][:, k, :], qraw[:, k, :], ACT.Copy, scale=wscale[:, k:k + 1]).then_inc(a_wq, 1)

        def keys_hi():
            act.wait_ge(t_keys, 1)
            act.wait_ge(v_zero, 2)
            for h2 in range(2):
                for h in range(HG):
                    r = slice(h * D, (h + 1) * D)
                    i = act.activation(kbd[HI][r, :, 2 * h2:2 * h2 + 2, h * M:(h + 1) * M].rearrange("p b g m -> p g b m"),
                                       bank[4 + h2][r, 0:4 * M].rearrange("p (g b m) -> p g b m", g=2, b=B), ACT.Copy)
            i.then_inc(a_keys, 1)

        def values_hi():
            act.wait_ge(t_vals, 1)
            for b in range(B):
                i = act.activation(vtok[HI][0:M, b, :], bank[6 + b][0:M, :], ACT.Copy)
            i.then_inc(a_vals, 1)
            act.wait_ge(d_pw, 16)
            act.activation(wp[HI][:, :, :], praw[:, :, :], ACT.Copy).then_inc(a_wp, 1)

        def step(k, back=False, scores=False, front=False, norm=False, keys_too=False, values_too=False, tail=False):
            b, s, f = k, k.plus(1), k.plus(2)

            def x_hi(t):
                t_xT.wait(act, f, t)
                t_q.wait(act, f.plus(-1), UT - 1)
                act.activation(xT[HI][:, :, t * P:(t + 1) * P], bA[t][:, :].rearrange("p (k n) -> p k n", k=KT),
                               ACT.Copy).then_inc(a_xT.sem, 1)

            def q_hi(h):
                t_q.wait(act, f, h)
                for m in (2 * h, 2 * h + 1):
                    i = act.activation(qT[HI][:, m, :], bA[h][:, (m % 2) * UN:(m % 2 + 1) * UN], ACT.Identity,
                                       bias=qbias[:, m:m + 1])
                i.then_inc(a_q.sem, 1)

            def prob_hi(g_):
                for t in range(UT):
                    i = g_ * UT + t
                    if t == 0:
                        t_av.wait(act, b, g_ - 2)
                    t_probT.wait(act, b, i)
                    act.activation(PT[HI][:, g_ % 2, :, t * P:(t + 1) * P],
                                   bT[i % 2][:, 0:NC * P].rearrange("p (c n) -> p c n", c=NC),
                                   ACT.Copy).then_inc(a_probT.sem, 1)

            def av_hi(g_):
                if g_ == 0:
                    t_proj.wait(act, b.plus(-1), UT - 1)
                t_av.wait(act, b, g_)
                act.activation(aT[HI][:, g_, :], bV[g_ % 2][:, 0:UN], ACT.Copy).then_inc(a_av.sem, 1)

            def exps(t, lo, hi):
                if lo == 0:
                    v_max.wait(act, s, t)
                for h in range(lo, hi):
                    v = S[:, s.u, t, h * M:(h + 1) * M]
                    i = act.activation(v, v, ACT.Exp, bias=nmax[:, s.u, t, h:h + 1],
                                       accum_out=esum[:, s.u, t, h:h + 1])
                if hi == H:
                    i.then_inc(a_exp.sem, 1)

            def exp_all(t):
                p_less.wait(act, s, 0)
                v = S[:, s.u, t, :]
                act.activation(v, v, ACT.Exp).then_inc(a_exp.sem, 1)

            if front:
                x_hi(0)
                x_hi(1)
            if back:
                prob_hi(0)
            if tail:
                w1_hi(0)
            if back:
                prob_hi(1)
            if tail:
                h_hi(static(0), 0)
            if scores:
                exps(0, 0, 4)
            if front:
                q_hi(0)
            if back:
                av_hi(0)
                prob_hi(2)
            if tail:
                h_hi(static(0), 1)
            if scores:
                exps(0, 4, 8)
            if back:
                av_hi(1)
                prob_hi(3)
            if tail:
                h_hi(static(0), 2)
            if scores:
                exps(0, 8, 11)
            if back:
                av_hi(2)
            if tail:
                h_hi(static(0), 3)
            if scores:
                exp_all(1)
            if front:
                q_hi(1)
            if back:
                av_hi(3)
            if values_too:
                values_hi()
            if scores:
                exps(0, 11, 16)
            if keys_too:
                keys_hi()

        def w1_hi(j):
            act.wait_ge(d_w1[j % 2], 16 * (j // 2) + 16)
            if j == 0:
                t_scores.wait(act, last_unit, UT * KT - 1)
            if j == JT - 3:
                t_proj.wait(act, last_unit, UT - 1)
            for k in range(KT):
                i = act.activation(w1[:, j, HI, k, :], w1raw[:, j % 2, k, :], ACT.Copy, scale=cols[:, N2W + k:N2W + k + 1])
            i.then_inc(a_w1, 1)

        def w2_hi(j):
            act.wait_ge(d_w2[j % 2], 16 * (j // 2) + 16)
            if j == 0:
                t_proj.wait(act, last_unit, UT - 1)
            act.activation(w2[:, j, HI, :], w2raw[:, j % 2, :], ACT.Copy).then_inc(a_w2, 1)

        def h_hi(n, t):
            t_hT.wait(act, n, t)
            act.activation(hT[n.u][HI][:, :, t * P:(t + 1) * P],
                           h_bank(n, t)[:, :].rearrange("p (k n) -> p k n", k=KT), ACT.Copy).then_inc(a_hT.sem, 1)

        pipeline(act, step)

        def step2(s, first=False, last=False):
            if first:
                w1_hi(1)
                w2_hi(0)
                w2_hi(1)
            for j in range(JT):
                t_fc1.wait(act, s, j)
                v_glo.wait(act, s, j - 1)
                act.activation(g[:, :], bF[j % 2][:, :], ACT.Gelu, bias=fc1_bias[:, j:j + 1]).then_inc(a_gelu.sem, 1)
                if first and j + 2 < JT:
                    w1_hi(j + 2)
                    w2_hi(j + 2)
                if not last and j - 1 in NORMS:
                    h_hi(s.plus(1), NORMS.index(j - 1))

        blocks(act, step2)

    def vector_program(dve):
        for c in counts1:
            dve.sem_inc(c.sem, c.start)

        for t in kbd:
            dve.memset(f32(t[:, :, :, :]).rearrange("p a b c -> p (a b c)"), 0.0).then_inc(v_zero, 1)
        dve.wait_ge(d_ctx, 16)
        for b in range(B):
            i = dve.bn_stats(cbn[0:M, b, :], cx[0:M, b, :])
        i.then_inc(s_chain, 1)
        dve.wait_ge(s_chain, 1)
        for b in range(B):
            i = dve.bn_aggr(cmv[0:M, b, :], cbn[0:M, b, :])
        i.then_inc(s_chain, 1)
        dve.wait_ge(s_chain, 2)
        dve.tensor_scalar(cve[0:M, :], cmv[0:M, :, 1], EPS, None, ALU.add).then_inc(v_cve, 1)
        dve.wait_ge(t_cols, 1)
        dve.tensor_copy(cols[:, :], bank[7][:, 0:40]).then_inc(v_cols, 1)
        dve.wait_ge(v_cols, 1)
        dve.tensor_scalar(wscale[:, :], cols[:, QNW:QNW + KT], SCALE, None, ALU.mult).then_inc(v_wscale, 1)
        dve.wait_ge(p_crs, 1)
        for b in range(B):
            i = dve.tensor_scalar(cx[0:M, b, :], cx[0:M, b, :], cmv[0:M, b, 0:1], crs[0:M, b:b + 1],
                                  ALU.subtract, ALU.mult)
        i.then_inc(v_ctx, 1)

        def q_weights():
            dve.wait_ge(t_ctxT, 1)
            for b in range(B):
                for k in range(KT):
                    i = dve.tensor_scalar(cxT[:, k, b, :], bank[2 + b][:, k * M:(k + 1) * M],
                                          cols[:, CNW + k:CNW + k + 1], cols[:, CNB + k:CNB + k + 1], ALU.mult, ALU.add)
            i.then_inc(v_ctxT, 1)
            dve.wait_ge(v_wscale, 1)
            for k in range(KT):
                dve.wait_ge(a_wq, k + 1)
                i = dve.scalar_tensor_tensor(out=wq[LO][:, k, :], in0=qraw[:, k, :], scalar=wscale[:, k:k + 1],
                                             in1=f32(wq[HI][:, k, :]), op0=ALU.mult, op1=ALU.subtract)
            i.then_inc(v_wq, 1)
            dve.wait_ge(t_qbias, 1)
            dve.tensor_scalar(qbias[:, :], bank[6][:, 0:KT], SCALE, None, ALU.mult).then_inc(v_qbias, 1)

        def keys_lo():
            dve.wait_ge(a_keys, 1)
            for h2 in range(2):
                for h in range(HG):
                    r = slice(h * D, (h + 1) * D)
                    i = dve.tensor_tensor(*(kbd[part][r, :, 2 * h2:2 * h2 + 2, h * M:(h + 1) * M].rearrange(
                        "p b g m -> p g b m") if part == LO else
                        bank[4 + h2][r, 0:4 * M].rearrange("p (g b m) -> p g b m", g=2, b=B) for part in (LO, HI)),
                        f32(kbd[HI][r, :, 2 * h2:2 * h2 + 2, h * M:(h + 1) * M]).rearrange("p b g m -> p g b m"),
                        ALU.subtract)
            i.then_inc(v_keys, 1)

        def values_lo():
            dve.wait_ge(a_vals, 1)
            for b in range(B):
                i = dve.tensor_tensor(vtok[LO][0:M, b, :], bank[6 + b][0:M, :], f32(vtok[HI][0:M, b, :]), ALU.subtract)
            i.then_inc(v_vals, 1)
            dve.wait_ge(a_wp, 1)
            dve.tensor_tensor(wp[LO][:, :, :], praw[:, :, :], f32(wp[HI][:, :, :]), ALU.subtract).then_inc(v_wp, 1)

        def step(k, back=False, scores=False, front=False, norm=False, keys_too=False, values_too=False, tail=False):
            b, s, f, n = k, k.plus(1), k.plus(2), k.plus(3)

            def masked(t, g_):
                i = t * KT + g_
                if i == 0:
                    p_neg.wait(dve, s, 0)
                    t_probT.wait(dve, s.plus(-2), KT * UT - 1)
                t_scores.wait(dve, s, i)
                dve.tensor_tensor(S[:, s.u, t, g_ * GM:(g_ + 1) * GM].rearrange("p (h m) -> p h m", h=HG),
                                  bS[i % 2][:, 0:GM].rearrange("p (h m) -> p h m", h=HG),
                                  negm[:, s.u, t, :].unsqueeze(1).to_broadcast([P, HG, M]),
                                  ALU.add).then_inc(v_scores.sem, 1)

            def maximum(t):
                v_scores.wait(dve, s, (t + 1) * KT - 1)
                dve.tensor_reduce(nmax[:, s.u, t, :], S[:, s.u, t, :].rearrange("p (h m) -> p h m", h=H), AX.X,
                                  ALU.max, negate=True).then_inc(v_max.sem, 1)

            def x_lo(t):
                a_xT.wait(dve, f, t)
                v = slice(t * P, (t + 1) * P)
                dve.tensor_tensor(xT[LO][:, :, v], bA[t][:, :].rearrange("p (k n) -> p k n", k=KT),
                                  f32(xT[HI][:, :, v]), ALU.subtract).then_inc(v_xT.sem, 1)

            def q_lo(h):
                a_q.wait(dve, f, h)
                for m in (2 * h, 2 * h + 1):
                    i = dve.scalar_tensor_tensor(out=qT[LO][:, m, :], in0=bA[h][:, (m % 2) * UN:(m % 2 + 1) * UN],
                                                 scalar=qbias[:, m:m + 1], in1=f32(qT[HI][:, m, :]),
                                                 op0=ALU.add, op1=ALU.subtract)
                i.then_inc(v_q.sem, 1)

            def prob_lo(g_):
                for t in range(UT):
                    i = g_ * UT + t
                    v = slice(t * P, (t + 1) * P)
                    a_probT.wait(dve, b, i)
                    dve.tensor_tensor(PT[LO][:, g_ % 2, :, v],
                                      bT[i % 2][:, 0:NC * P].rearrange("p (c n) -> p c n", c=NC),
                                      f32(PT[HI][:, g_ % 2, :, v]), ALU.subtract).then_inc(v_probT.sem, 1)

            def av_lo(g_):
                a_av.wait(dve, b, g_)
                dve.tensor_tensor(aT[LO][:, g_, :], bV[g_ % 2][:, 0:UN], f32(aT[HI][:, g_, :]),
                                  ALU.subtract).then_inc(v_av.sem, 1)

            def exp_sum():
                a_exp.wait(dve, s, 0)
                dve.tensor_reduce(esum[:, s.u, 1, :], S[:, s.u, 1, :].rearrange("p (h m) -> p h m", h=H), AX.X,
                                  ALU.add).then_inc(v_esum.sem, 1)

            def recip(t):
                if t == 1:
                    v_esum.wait(dve, s, 0)
                else:
                    a_exp.wait(dve, s, 1)
                dve.reciprocal(rsum[:, s.u, t, :], esum[:, s.u, t, :]).then_inc(v_rsum.sem, 1)

            def stats():
                dve.wait_ge(d_x[n.u], n.q * 16 + 16)
                for t in range(UT):
                    dve.bn_stats(bnst[:, t, :], xr[:, bass.ds(n.slot(), 1), t, :]).then_inc(v_bn.sem, 1)

            def variance():
                for t in range(UT):
                    dve.bn_aggr(mv[:, t, :], bnst[:, t, :]).then_inc(v_mv.sem, 1)
                v_mv.wait(dve, n, UT - 1)
                dve.tensor_scalar(veps[:, :], mv[:, :, 1], EPS, None, ALU.add).then_inc(v_veps.sem, 1)

            def normed():
                p_rstd.wait(dve, n, 0)
                for t in range(UT):
                    t_xT.wait(dve, n.plus(-1), t)
                    dve.tensor_scalar(xhat[:, t:t + 1, :], xr[:, bass.ds(n.slot(), 1), t, :], mv[:, t, 0:1],
                                      rstd[:, t:t + 1], ALU.subtract, ALU.mult).then_inc(v_xhat.sem, 1)

            def residual(t):
                t_proj.wait(dve, b, t)
                p_projb.wait(dve, b, t)
                v = xr[:, bass.ds(b.slot(), 1), t, :]
                dve.tensor_tensor(v, bV[t][:, :].unsqueeze(1), v, ALU.add).then_inc(v_res.sem, 1)

            if keys_too:
                q_weights()
            if front:
                x_lo(0)
            if scores:
                masked(0, 0)
                masked(0, 1)
            if front:
                x_lo(1)
            if scores:
                masked(0, 2)
                masked(0, 3)
            if back:
                prob_lo(0)
            if tail:
                h_norm(static(0), 0)
                w1_lo(0)
            if scores:
                masked(1, 0)
                masked(1, 1)
                maximum(0)
            if back:
                prob_lo(1)
            if tail:
                h_lo(static(0), 0)
                h_norm(static(0), 1)
            if scores:
                masked(1, 2)
                masked(1, 3)
                maximum(1)
            if back:
                av_lo(0)
                prob_lo(2)
            if tail:
                h_lo(static(0), 1)
                h_norm(static(0), 2)
            if front:
                q_lo(0)
            if back:
                av_lo(1)
                prob_lo(3)
            if tail:
                h_lo(static(0), 2)
                h_norm(static(0), 3)
            if norm:
                stats()
            if back:
                av_lo(2)
            if tail:
                h_lo(static(0), 3)
            if norm:
                v_bn.wait(dve, n, UT - 1)
            if scores:
                exp_sum()
            if norm:
                variance()
            if front:
                q_lo(1)
            if back:
                av_lo(3)
            if scores:
                recip(1)
            if values_too:
                values_lo()
            if norm:
                normed()
            if back:
                residual(0)
            if scores:
                recip(0)
            if back:
                residual(1)
            if keys_too:
                keys_lo()

        def w1_lo(j):
            dve.wait_ge(t_bias, j + 1)
            dve.tensor_tensor(fc1_bias[:, j:j + 1], bias_bank(j)[:, j:j + 1], cols[:, F1B + j:F1B + j + 1],
                              ALU.add).then_inc(v_bias, 1)
            dve.wait_ge(a_w1, j + 1)
            for k in range(KT):
                i = dve.scalar_tensor_tensor(out=w1[:, j, LO, k, :], in0=w1raw[:, j % 2, k, :],
                                             scalar=cols[:, N2W + k:N2W + k + 1], in1=f32(w1[:, j, HI, k, :]),
                                             op0=ALU.mult, op1=ALU.subtract)
            i.then_inc(v_w1, 1)

        def w2_lo(j):
            dve.wait_ge(a_w2, j + 1)
            dve.tensor_tensor(w2[:, j, LO, :], w2raw[:, j % 2, :], f32(w2[:, j, HI, :]),
                              ALU.subtract).then_inc(v_w2, 1)

        def h_stats(n, t):
            if t == 0:
                dve.wait_ge(d_x2[n.u], n.q * 16 + 16)
            dve.bn_stats(hbn[:, :], x2[n.u][:, t, :]).then_inc(v_hbn.sem, 1)

        def h_variance(n, t):
            dve.bn_aggr(hmv[:, :], hbn[:, :]).then_inc(v_hmv.sem, 1)
            v_hmv.wait(dve, n, t)
            dve.tensor_scalar(hve[:, :], hmv[:, 1:2], EPS, None, ALU.add).then_inc(v_hve.sem, 1)

        def h_normed(n, t):
            p_hrs.wait(dve, n, t)
            t_hT.wait(dve, n, t - 1)
            dve.tensor_scalar(hhat[:, :], x2[n.u][:, t, :], hmv[:, 0:1], hrs[:, 0:1], ALU.subtract,
                              ALU.mult).then_inc(v_hhat.sem, 1)

        def h_norm(n, t):
            h_stats(n, t)
            v_hbn.wait(dve, n, t)
            h_variance(n, t)
            h_normed(n, t)

        def h_lo(n, t):
            a_hT.wait(dve, n, t)
            v = slice(t * P, (t + 1) * P)
            dve.tensor_tensor(hT[n.u][LO][:, :, v], h_bank(n, t)[:, :].rearrange("p (k n) -> p k n", k=KT),
                              f32(hT[n.u][HI][:, :, v]), ALU.subtract).then_inc(v_hT.sem, 1)

        pipeline(dve, step)

        def step2(s, first=False, last=False):
            def output(n, t):
                t_fc2.wait(dve, n, (JT - 1) * ST + t)
                p_fc2b.wait(dve, n, t)
                dve.tensor_tensor(x2[n.u][:, t, :], bC[t][:, :], x2[n.u][:, t, :], ALU.add).then_inc(v_out.sem, 1)

            if first:
                w1_lo(1)
                w2_lo(0)
                w2_lo(1)
            for j in range(JT):
                a_gelu.wait(dve, s, j)
                t_fc2.wait(dve, s, (j - 3) * ST - 1)
                dve.tensor_copy(gT[HI][:, j % 4, :], g[:, :]).then_inc(v_ghi.sem, 1)
                norming = not last and j in NORMS
                if norming:
                    h_stats(s.plus(1), NORMS.index(j))
                    v_hbn.wait(dve, s.plus(1), NORMS.index(j))
                v_ghi.wait(dve, s, j)
                dve.tensor_tensor(gT[LO][:, j % 4, :], g[:, :], f32(gT[HI][:, j % 4, :]),
                                  ALU.subtract).then_inc(v_glo.sem, 1)
                if first and j + 2 < JT:
                    w1_lo(j + 2)
                    w2_lo(j + 2)
                if not first and j == 1:
                    for t in range(ST):
                        output(s.plus(-1), t)
                if not last and j - 2 in NORMS:
                    h_lo(s.plus(1), NORMS.index(j - 2))
                if norming:
                    h_variance(s.plus(1), NORMS.index(j))
                    h_normed(s.plus(1), NORMS.index(j))
            if last:
                for t in range(ST):
                    output(s, t)

        blocks(dve, step2)

    def tensor_program(pe):
        pe.wait_ge(d_rows, 16 * 7)
        pe.wait_ge(p_ident, 2)
        pe.transpose(bank[7][:, 0:40], rows[:, :], ident[0:40, 0:40]).then_inc(t_cols, 1)
        pe.wait_ge(v_ctx, 1)
        for b in range(B):
            for k in range(KT):
                i = pe.transpose(bank[2 + b][:, k * M:(k + 1) * M], cx[0:M, b, k * P:(k + 1) * P], ident[0:M, 0:M])
        i.then_inc(t_ctxT, 1)

        def q_bias():
            pe.wait_ge(v_cols, 1)
            pe.wait_ge(d_qw, 16)
            for m in range(KT):
                for k in range(KT):
                    i = pe.matmul(bank[6][:, m:m + 1], qraw[:, k, m * P:(m + 1) * P], cols[:, QNB + k:QNB + k + 1],
                                  start=(k == 0), stop=(k == KT - 1))
            i.then_inc(t_qbias, 1)

        def keys():
            pe.wait_ge(v_ctxT, 1)
            pe.wait_ge(d_kw, 16)
            for g_ in range(KT):
                for k in range(KT):
                    i = pe.matmul(bank[4 + g_ // 2][:, (g_ % 2) * B * M:(g_ % 2 + 1) * B * M],
                                  kvw[:, k, g_ * P:(g_ + 1) * P], cxT[:, k, :, :].rearrange("p b m -> p (b m)"),
                                  start=(k == 0), stop=(k == KT - 1))
            i.then_inc(t_keys, 1)
            pe.wait_ge(v_keys, 1)

        def values():
            pe.wait_ge(d_vw, 16)
            pe.wait_ge(v_qbias, 1)
            for b in range(B):
                for k in range(KT):
                    i = pe.matmul(bank[6 + b][0:M, :], cxT[:, k, b, :], kvw[:, k, C:2 * C],
                                  start=(k == 0), stop=(k == KT - 1))
            i.then_inc(t_vals, 1)

        def step(k, back=False, scores=False, front=False, norm=False, keys_too=False, values_too=False, tail=False):
            b, s, f = k, k.plus(1), k.plus(2)

            def score(t, g_):
                i = t * KT + g_
                if i == 0:
                    v_q.wait(pe, s, UT - 1)
                v_scores.wait(pe, s, i - 2)
                for n, (w, d) in enumerate(PRODUCTS):
                    mm = pe.matmul(bS[i % 2][:, 0:GM], qT[d][:, g_, t * P:(t + 1) * P], kbd[w][:, s.u, g_, :],
                                   start=(n == 0), stop=(n == 2))
                mm.then_inc(t_scores.sem, 1)

            def x_T(t):
                v_xhat.wait(pe, f, t)
                v_q.wait(pe, f.plus(-1), t)
                for c in range(KT):
                    mm = pe.transpose(bA[t][:, c * P:(c + 1) * P], xhat[:, t, c * P:(c + 1) * P], ident[:, :])
                mm.then_inc(t_xT.sem, 1)

            def q(m):
                if m == 0:
                    v_xT.wait(pe, f, UT - 1)
                n = 0
                for c in range(KT):
                    for w, d in PRODUCTS:
                        mm = pe.matmul(bA[m // 2][:, (m % 2) * UN:(m % 2 + 1) * UN], wq[w][:, c, m * P:(m + 1) * P],
                                       xT[d][:, c, :], start=(n == 0), stop=(n == 3 * KT - 1))
                        n += 1
                if m % 2:
                    mm.then_inc(t_q.sem, 1)

            def prob_T(g_):
                for t in range(UT):
                    i = g_ * UT + t
                    if g_ == 0:
                        p_prob.wait(pe, b, UT - 1)
                    v_probT.wait(pe, b, i - 2)
                    for c in range(NC):
                        r = g_ * GM + CH0[c]
                        mm = pe.transpose(bT[i % 2][:, c * P:(c + 1) * P], S[:, b.u, t, r:r + P], ident[:, :])
                    mm.then_inc(t_probT.sem, 1)

            def av(g_):
                v_probT.wait(pe, b, g_ * UT + UT - 1)
                if g_ < 2:
                    v_res.wait(pe, b.plus(-1), g_)
                else:
                    v_av.wait(pe, b, g_ - 2)
                n = 0
                for c in range(NC):
                    for w, d in PRODUCTS:
                        mm = pe.matmul(bV[g_ % 2][:, 0:UN], vbd[w][:, b.u, g_ * NC + c, :], PT[d][:, g_ % 2, c, :],
                                       start=(n == 0), stop=(n == 3 * NC - 1))
                        n += 1
                mm.then_inc(t_av.sem, 1)

            def proj(t):
                n = 0
                for c in range(KT):
                    if t == 0 and c in (0, KT - 1):
                        v_av.wait(pe, b, KT - 2 + (c > 0))
                    for w, d in PRODUCTS:
                        mm = pe.matmul(bV[t][:, :], aT[d][:, c, t * P:(t + 1) * P], wp[w][:, c, :],
                                       start=(n == 0), stop=(n == 3 * KT - 1))
                        n += 1
                mm.then_inc(t_proj.sem, 1)

            if front:
                x_T(0)
                x_T(1)
            if keys_too:
                q_bias()
                pe.wait_ge(v_wq, 1)
            if scores:
                for g_ in range(KT):
                    score(0, g_)
            if back:
                prob_T(0)
            if tail:
                bias(0)
                bias(1)
            if front:
                q(0)
            if scores:
                score(1, 0)
                score(1, 1)
            if back:
                prob_T(1)
            if tail:
                h_T(static(0), 0)
            if front:
                q(1)
            if scores:
                score(1, 2)
                score(1, 3)
            if values_too:
                values()
            if back:
                av(0)
                prob_T(2)
            if tail:
                h_T(static(0), 1)
            if front:
                q(2)
            if back:
                av(1)
                prob_T(3)
            if tail:
                h_T(static(0), 2)
            if back:
                av(2)
            if tail:
                h_T(static(0), 3)
            if front:
                q(3)
            if back:
                av(3)
                proj(0)
                proj(1)
            if keys_too:
                keys()
            if values_too:
                pe.wait_ge(v_vals, 1)
                pe.wait_ge(v_wp, 1)
                for b in range(B):
                    pe.wait_ge(d_vbd[b], 16 * 12)

        def bias(j):
            pe.wait_ge(d_w1[j % 2], 16 * (j // 2) + 16)
            if j == 0:
                v_scores.wait(pe, last_unit, UT * KT - 1)
            if j >= 2:
                pe.wait_ge(v_bias, j)
            for k in range(KT):
                mm = pe.matmul(bias_bank(j)[:, j:j + 1], w1raw[:, j % 2, k, :], cols[:, N2B + k:N2B + k + 1],
                               start=(k == 0), stop=(k == KT - 1))
            mm.then_inc(t_bias, 1)

        def h_T(n, t):
            v_hhat.wait(pe, n, t)
            v_hT.wait(pe, n, t - (1 if h_bank(n, t) is bX else 2))
            for c in range(KT):
                mm = pe.transpose(h_bank(n, t)[:, c * P:(c + 1) * P], hhat[:, c * P:(c + 1) * P], ident[:, :])
            mm.then_inc(t_hT.sem, 1)

        pe.wait_ge(v_cols, 1)
        pipeline(pe, step)

        def step2(s, first=False, last=False):
            def fc1(j):
                if first:
                    pe.wait_ge(v_w1, j + 1)
                    if j == 0:
                        pe.wait_ge(v_bias, 2)
                if j == 0:
                    v_hT.wait(pe, s, ST - 1)
                a_gelu.wait(pe, s, j - 2)
                n = 0
                for c in range(KT):
                    for w, d in PRODUCTS:
                        mm = pe.matmul(bF[j % 2][:, :], w1[:, j, w, c, :], hT[s.u][d][:, c, :],
                                       start=(n == 0), stop=(n == 3 * KT - 1))
                        n += 1
                mm.then_inc(t_fc1.sem, 1)

            def fc2(n, j):
                if first:
                    pe.wait_ge(v_w2, j + 1)
                v_glo.wait(pe, n, j)
                for t in range(ST):
                    if j == 0:
                        v_out.wait(pe, n.plus(-1), t)
                    for i, (w, d) in enumerate(PRODUCTS):
                        mm = pe.matmul(bC[t][:, :], gT[d][:, j % 4, t * P:(t + 1) * P], w2[:, j, w, :],
                                       start=(j == 0 and i == 0), stop=(j == JT - 1 and i == 2))
                    mm.then_inc(t_fc2.sem, 1)

            if first:
                v_res.wait(pe, last_unit, UT - 1)
            for j in range(JT):
                fc1(j)
                if first and j + 2 < JT:
                    bias(j + 2)
                if j >= 2:
                    fc2(s, j - 2)
                elif not first:
                    fc2(s.plus(-1), JT - 2 + j)
                if not last and j - 1 in NORMS:
                    h_T(s.plus(1), NORMS.index(j - 1))
            if first:
                pe.wait_ge(v_w2, JT)
            if last:
                fc2(s, JT - 2)
                fc2(s, JT - 1)

        blocks(pe, step2)

    with nc.Block() as block:
        block.sync(sync_program)
        block.gpsimd(gpsimd_program)
        block.scalar(scalar_program)
        block.vector(vector_program)
        block.tensor(tensor_program)


INPUTS = ["x", "ctx_1024", "mask_BxSxS2_bk0"] + [
    f"L0_xattn_{n}" for n in ("qn_w", "qn_b", "cn_w", "cn_b", "n2_w", "n2_b", "q_w", "kv_w", "proj_w", "proj_b",
                              "fc1_w", "fc1_b", "fc2_w", "fc2_b")]


def kernel(**inputs):
    import numpy as np
    import concourse.bacc as bacc
    from concourse.bass_utils import run_bass_kernel_spmd

    nc = bacc.Bacc("TRN2", target_bir_lowering=False, num_devices=1)
    arrays, args = {}, []
    for name in INPUTS:
        a = np.ascontiguousarray(inputs[name])
        arrays[f"in_{name}"] = a
        args.append(nc.dram_tensor(f"in_{name}", a.shape, mybir.dt.from_np(a.dtype), kind="ExternalInput").ap())
    args.append(nc.dram_tensor("out_0", inputs["x"].shape, F32, kind="ExternalOutput").ap())
    build_block(nc, *args)
    return run_bass_kernel_spmd(nc, [arrays], core_ids=[0]).results[0]["out_0"]
```

```python
import concourse.bass as bass
from concourse import mybir

F32 = mybir.dt.float32
F32R = mybir.dt.float32r
U8 = mybir.dt.uint8
ALU = mybir.AluOpType
ACT = mybir.ActivationFunctionType
AX = mybir.AxisListType

P = 128
EPS = 1e-5
FLT_MAX = 3.4028234663852886e38
HI, LO = 0, 1
PRODUCTS = ((HI, HI), (LO, HI), (HI, LO))


class Unit:

    def __init__(self, q, u):
        self.q, self.u = q, u

    def plus(self, d):
        return Unit(self.q + (self.u + d) // 2, (self.u + d) % 2)

    def slot(self):
        return (self.q % 2) * 2 + self.u


class Count:

    def __init__(self, nc, name, per, start=0):
        self.sem, self.per, self.start = nc.alloc_semaphore(name), per, start

    def after(self, unit, i):
        return unit.q * (2 * self.per) + (unit.u * self.per + self.start + i + 1)

    def wait(self, eng, unit, i):
        value = self.after(unit, i)
        if isinstance(value, int) and value <= self.start:
            return
        eng.wait_ge(self.sem, value)


def build_block(nc, x, ctx, mask, qn_w, qn_b, cn_w, cn_b, n2_w, n2_b, q_w, kv_w, proj_w, proj_b,
                fc1_w, fc1_b, fc2_w, fc2_b, out):
    B, N, C = x.shape
    M = ctx.shape[1]
    HID = fc1_w.shape[1]
    H = 16
    D = C // H
    SCALE = D ** -0.5
    KT = C // P
    HG = P // D
    GM = HG * M
    UT = 2
    UN = UT * P
    NU = B * N // UN
    NC = -(-GM // P)
    CH0 = [c * (GM - P) // (NC - 1) for c in range(NC)]
    CH0[-1] = GM - P
    SB = 512
    ST = SB // P
    NS = B * N // SB
    JT = HID // P
    assert B == 2 and N % UN == 0 and NU % 2 == 0 and NU >= 8 and NS % 2 == 0 and NS >= 4

    x_v = x.rearrange("b (n t p) c -> b p n t c", t=UT, p=P)
    mask_v = mask.rearrange("b (n t p) m -> b p n t m", t=UT, p=P)
    x2_dram = nc.dram_tensor("x2_scratch", [B * N, C], F32, kind="Internal").ap()
    x2_units = x2_dram.rearrange("(b n t p) c -> b p n t c", b=B, t=UT, p=P)
    x2_blocks = x2_dram.rearrange("(s t p) c -> p s t c", t=ST, p=P)
    out_blocks = out.rearrange("b n c -> (b n) c").rearrange("(s t p) c -> p s t c", t=ST, p=P)
    fc1_v = fc1_w.rearrange("(k p) (j n) -> j p k n", p=P, n=P)
    fc2_v = fc2_w.rearrange("(j p) n -> j p n", p=P)

    base = 16512
    top = [base]

    def at(name, shape, dt, offset=None):
        size = 1 if dt is U8 else 4
        for s in shape[1:]:
            size *= s
        if offset is None:
            offset = top[0]
            top[0] += (size + 31) // 32 * 32
        return nc.alloc_sbuf_tensor_at(name, shape, dt, offset=offset)

    ident = at("ident", [P, P], F32)
    cols = at("cols", [P, 40], F32)
    qbias = at("qbias", [P, KT], F32)
    mhalf = at("mhalf", [P, 4], F32)
    wscale = at("wscale", [P, KT], F32)
    region1 = top[0]

    wq = [at(f"wq{s}", [P, KT, C], F32R) for s in "hl"]
    kbd = [at(f"kbd{s}", [P, B, KT, GM], F32R) for s in "hl"]
    xT = [at(f"xT{s}", [P, KT, UN], F32R) for s in "hl"]
    qT = [at(f"qT{s}", [P, KT, UN], F32R) for s in "hl"]
    xhat = at("xhat", [P, UT, C], F32)
    wp = [at(f"wp{s}", [P, KT, C], F32R) for s in "hl"]
    vbd = [at(f"vbd{s}", [P, B, KT * NC, P], F32R) for s in "hl"]
    S = at("S", [P, 2, UT, H * M], F32)
    PT = [at(f"PT{s}", [P, 2, NC, UN], F32R) for s in "hl"]
    aT = [at(f"aT{s}", [P, KT, UN], F32R) for s in "hl"]
    xr = at("xr", [P, 4, UT, C], F32)
    projb = at("projb", [P, C], F32)
    mask_in = at("mask_in", [P, 2, UT, M], U8)
    negm = at("negm", [P, 2, UT, M], F32)
    bnst = at("bnst", [P, UT, 6], F32)
    mv = at("mv", [P, UT, 2], F32)
    veps = at("veps", [P, UT], F32)
    rstd = at("rstd", [P, UT], F32)
    region2 = top[0]

    kvw = at("kvw", [P, KT, 2 * C], F32)
    qraw = at("qraw", [P, KT, C], F32)
    praw = at("praw", [P, KT, C], F32)
    cx = at("cx", [P, B, C], F32)
    cxT = at("cxT", [P, KT, B, M], F32)
    vtok = [at(f"vtok{s}", [P, B, C], F32R) for s in "hl"]
    rows = at("rows", [40, P], F32)
    cbn = at("cbn", [P, B, 6], F32)
    cmv = at("cmv", [P, B, 2], F32)
    cve = at("cve", [P, B], F32)
    crs = at("crs", [P, B], F32)
    end0 = top[0]

    top[0] = region2
    x2_0 = at("x2_0", [P, ST, C], F32)
    hT_0 = [at(f"hT0{s}", [P, KT, SB], F32R) for s in "hl"]
    w1raw = at("w1raw", [P, 2, KT, P], F32)
    w2raw = at("w2raw", [P, 2, C], F32)
    hhat = at("hhat", [P, C], F32)
    fc2b = at("fc2b", [P, C], F32)
    gT_start = top[0]
    gT = [at(f"gT{s}", [P, 4, SB], F32R) for s in "hl"]
    gT_end = top[0]
    hbn = at("hbn", [P, 6], F32)
    hmv = at("hmv", [P, 2], F32)
    hve = at("hve", [P, 1], F32)
    hrs = at("hrs", [P, 1], F32)
    end2 = top[0]
    top[0] = max(end0, gT_start)
    nmax = at("nmax", [P, 2, UT, H], F32)
    esum = at("esum", [P, 2, UT, H], F32)
    rsum = at("rsum", [P, 2, UT, H], F32)
    assert top[0] <= gT_end, (top[0], gT_start, gT_end, end0)
    top[0] = region1
    w1 = at("w1", [P, JT, 2, KT, P], F32R)
    w2 = at("w2", [P, JT, 2, C], F32R)
    x2_1 = at("x2_1", [P, ST, C], F32)
    hT_1 = [at(f"hT1{s}", [P, KT, SB], F32R) for s in "hl"]
    g = at("g", [P, SB], F32)
    assert top[0] <= region2 and max(end0, end2) <= 229344, (top[0], region2, end0, end2)
    x2 = [x2_0, x2_1]
    hT = [hT_0, hT_1]

    QNW, QNB, CNW, CNB, N2W, N2B, F1B = (4 * i for i in range(7))

    bank = [nc.alloc_psum_tensor(f"bank{i}", [P, 512], F32) for i in range(8)]
    bA, bS, bT, bV = bank[0:2], bank[2:4], bank[4:6], bank[6:8]
    bC, bF, bX = [bank[i] for i in (2, 3, 6, 7)], bank[0:2], bank[4]

    def sem(name):
        return nc.alloc_semaphore(name)

    d_rows, d_ctx, d_kw, d_vw, d_qw, d_pw, d_projb = (sem(f"d_{n}") for n in
                                                      ("rows", "ctx", "kw", "vw", "qw", "pw", "projb"))
    d_vbd = [sem("d_vbd0"), sem("d_vbd1")]
    d_x = [sem("d_x0"), sem("d_x1")]
    d_mask = [sem("d_mask0"), sem("d_mask1")]
    d_x2st = sem("d_x2st")
    p_ident, p_half, p_zero, p_crs = (sem(f"p_{n}") for n in ("ident", "half", "zero", "crs"))
    t_cols, v_cols, v_cve, v_ctx, t_ctxT, v_ctxT = (sem(n) for n in
                                                    ("t_cols", "v_cols", "v_cve", "v_ctx", "t_ctxT", "v_ctxT"))
    t_keys, a_keys, v_keys, t_vals, a_vals, v_vals = (sem(n) for n in
                                                      ("t_keys", "a_keys", "v_keys", "t_vals", "a_vals", "v_vals"))
    t_qbias, v_qbias, v_wscale, a_wq, v_wq, a_wp, v_wp = (sem(n) for n in ("t_qbias", "v_qbias", "v_wscale", "a_wq",
                                                                           "v_wq", "a_wp", "v_wp"))

    def count(name, per, start=0):
        return Count(nc, name, per, start)

    t_scores = count("t_scores", UT * KT)
    v_scores = count("v_scores", UT * KT, 2)
    v_max = count("v_max", UT)
    a_exp = count("a_exp", UT)
    v_rsum = count("v_rsum", UT)
    p_prob = count("p_prob", UT)
    t_probT = count("t_probT", KT * UT, 1)
    a_probT = count("a_probT", KT * UT)
    v_probT = count("v_probT", KT * UT, 2)
    t_av = count("t_av", KT, 2)
    a_av = count("a_av", KT)
    v_av = count("v_av", KT)
    t_proj = count("t_proj", UT, 1)
    v_res = count("v_res", UT, 2)
    t_xT = count("t_xT", UT)
    a_xT = count("a_xT", UT)
    v_xT = count("v_xT", UT)
    t_q = count("t_q", UT, 1)
    a_q = count("a_q", UT)
    v_q = count("v_q", UT, 2)
    v_bn, v_mv, v_veps = count("v_bn", UT), count("v_mv", UT), count("v_veps", 1)
    p_rstd = count("p_rstd", 1)
    v_xhat = count("v_xhat", UT)
    p_projb = count("p_projb", UT)
    p_neg = count("p_neg", 1)
    counts1 = [v_scores, t_probT, v_probT, t_av, t_proj, v_res, t_q, v_q]

    d_w1 = [sem("d_w1_0"), sem("d_w1_1")]
    d_w2 = [sem("d_w2_0"), sem("d_w2_1")]
    d_fc2b, d_out = sem("d_fc2b"), sem("d_out")
    d_x2 = [sem("d_x2_0"), sem("d_x2_1")]
    a_w1, v_w1, a_w2, v_w2 = (sem(n) for n in ("a_w1", "v_w1", "a_w2", "v_w2"))
    v_hbn, v_hmv, v_hve = count("v_hbn", ST), count("v_hmv", ST), count("v_hve", ST)
    p_hrs, v_hhat = count("p_hrs", ST), count("v_hhat", ST)
    t_hT, a_hy, a_hT, v_hT = count("t_hT", ST), count("a_hy", ST), count("a_hT", ST), count("v_hT", ST)
    t_fc1 = count("t_fc1", JT)
    a_gelu = count("a_gelu", JT)
    v_ghi = count("v_ghi", JT)
    v_glo = count("v_glo", JT)
    t_fc2 = count("t_fc2", JT * ST)
    v_out = count("v_out", ST)
    p_fc2b = count("p_fc2b", ST)

    def f32(ap):
        return ap.bitcast(F32)

    def units(lo, hi, eng, body):
        with eng.Fori(lo // 2, hi // 2) as q:
            for u in range(2):
                body(Unit(q, u))

    def static(n):
        return Unit(n // 2, n % 2)

    LOOP = (0, NU - 6)

    NORM2 = {NU - 6 + t: t for t in range(ST)}
    SPLIT = {NU - 2: (0, 1), NU - 1: (2, 3)}
    W1_AHEAD = 4

    def pipeline(eng, step):
        step(static(-3), norm=True)
        step(static(-2), front=True, norm=True, prep="q")
        step(static(-1), scores=True, front=True, norm=True, prep="scores")
        units(*LOOP, eng, lambda k: step(k, back=True, scores=True, front=True, norm=True))
        for n in range(LOOP[1], NU):
            step(static(n), back=True, scores=n + 1 < NU, front=n + 2 < NU, norm=n + 3 < NU,
                 norm2=NORM2.get(n), split=SPLIT.get(n, ()))

    NORMS = [5 + 2 * t for t in range(ST)]
    assert NORMS[-1] + 2 < JT

    def blocks(eng, step):
        step(static(0), first=True)
        with eng.Fori(0, (NS - 2) // 2) as i:
            step(Unit(i, 1))
            step(Unit(i + 1, 0))
        step(static(NS - 1), last=True)

    last_unit = static(NU - 1)
    a_ctxT = sem("a_ctxT")
    s_chain = sem("v_chain")
    v_zero = sem("v_zero")
    p_less = count("p_less", 1)
    v_esum = count("v_esum", 1)

    def h_bank(n, t):
        return bA[0] if isinstance(n.q, int) and n.q == 0 and n.u == 0 else bX

    def load_row(eng, i):
        v = (qn_w, qn_b, cn_w, cn_b, n2_w, n2_b, fc1_b)[i]
        eng.dma_start(rows[4 * i:4 * i + v.shape[0] // P, :], v.rearrange("(k p) -> k p", p=P)).then_inc(d_rows, 16)

    def sync_program(sp):
        def load_x(n):
            sp.dma_start(xr[:, bass.ds(n.slot(), 1), :, :],
                         x_v[n.u][:, bass.ds(n.q, 1), :, :]).then_inc(d_x[n.u], 16)

        def load_mask(n):
            sp.dma_start(mask_in[:, n.u:n.u + 1, :, :],
                         mask_v[n.u][:, bass.ds(n.q, 1), :, :]).then_inc(d_mask[n.u], 16)

        sp.dma_start(cx[0:M, :, :], ctx.rearrange("b m c -> m b c")).then_inc(d_ctx, 16)
        for i in range(4):
            load_row(sp, i)
        load_x(static(0))
        load_mask(static(0))
        load_mask(static(1))
        sp.dma_start(projb[:, :], proj_b.rearrange("(a c) -> a c", a=1).to_broadcast([P, C])).then_inc(d_projb, 16)
        sp.wait_ge(d_x[0], 16)
        load_x(static(1))
        load_x(static(2))
        sp.wait_ge(d_x[1], 16)
        load_x(static(3))
        for n in (2, 3):
            p_neg.wait(sp, static(n - 2), 0)
            load_mask(static(n))
        sp.wait_ge(p_zero, 2)
        for b, part, h, c in ((b, part, h, c) for b in range(B) for part in (HI, LO) for h in range(HG) for c in range(NC)):
            if (part, h, c) == (HI, 0, 0):
                sp.wait_ge(v_vals, b + 1)
            own = 0 if c == 0 else CH0[c - 1] + P
            r0, r1 = max(h * M, own), min((h + 1) * M, CH0[c] + P)
            if r0 < r1:
                sp.dma_start(
                    f32(vbd[part][r0 - CH0[c]:r1 - CH0[c], b, :, :]).rearrange("p (g c) n -> p g c n", c=NC)[
                        :, :, c, h * D:(h + 1) * D],
                    f32(vtok[part][r0 - h * M:r1 - h * M, b, :]).rearrange("p (g n) -> p g n", g=KT)[
                        :, :, h * D:(h + 1) * D]).then_inc(d_vbd[b], 16)
        def step(k, more=True):
            v_res.wait(sp, k, UT - 1)
            sp.dma_start(x2_units[k.u][:, bass.ds(k.q, 1), :, :],
                         xr[:, bass.ds(k.slot(), 1), :, :]).then_inc(d_x2st, 16)
            if more:
                sp.wait_ge(d_x2st, k.q * 32 + (k.u * 16 + 16))
                load_x(k.plus(4))
                load_mask(k.plus(4))

        units(0, NU - 8, sp, step)

        def load_w1(j):
            if j >= 2:
                sp.wait_ge(v_w1, j - 1)
            sp.dma_start(w1raw[:, j % 2, :, :], fc1_v[j]).then_inc(d_w1[j % 2], 16)

        def load_w2(j):
            if j >= 2:
                sp.wait_ge(v_w2, j - 1)
            sp.dma_start(w2raw[:, j % 2, :], fc2_v[j]).then_inc(d_w2[j % 2], 16)

        def load_x2(s):
            sp.dma_start(x2[s.u][:, :, :].unsqueeze(1),
                         x2_blocks[:, bass.ds(s.q * 2 + s.u, 1), :, :]).then_inc(d_x2[s.u], 16)

        def store_out(s):
            v_out.wait(sp, s, ST - 1)
            sp.dma_start(out_blocks[:, bass.ds(s.q * 2 + s.u, 1), :, :],
                         x2[s.u][:, :, :].unsqueeze(1)).then_inc(d_out, 16)
            sp.wait_ge(d_out, s.q * 32 + (s.u * 16 + 16))

        load_x2(static(0))
        sp.dma_start(fc2b[:, :], fc2_b.rearrange("(a c) -> a c", a=1).to_broadcast([P, C])).then_inc(d_fc2b, 16)
        for j in range(2):
            load_w1(j)
            load_w2(j)
        for n in range(NU - 8, NU):
            if n in SPLIT:
                for j in SPLIT[n]:
                    load_w1(j + 2)
            step(static(n), more=n + 4 < NU)
        t_proj.wait(sp, last_unit, UT - 1)
        sp.wait_ge(d_x2st, 16 * NU)
        load_x2(static(1))
        for j in range(2, JT):
            load_w2(j)
            if j + W1_AHEAD < JT:
                load_w1(j + W1_AHEAD)
        store_out(static(0))
        load_x2(static(2))
        with sp.Fori(0, (NS - 2) // 2 - 1) as i:
            for s in (Unit(i, 1), Unit(i + 1, 0)):
                store_out(s)
                load_x2(s.plus(2))
        store_out(static(NS - 3))
        load_x2(static(NS - 1))
        store_out(static(NS - 2))
        for t in range(ST):
            v_out.wait(sp, static(NS - 1), t)
            sp.dma_start(out_blocks[:, NS - 1, t, :], x2[(NS - 1) % 2][:, t, :]).then_inc(d_out, 16)
        sp.wait_ge(d_out, 16 * (NS - 1 + ST))

    def gpsimd_program(pool):
        pool.memset(mhalf[:, :], -0.5).then_inc(p_half, 1)
        pool.memset(ident[:, :], 0.0).then_inc(p_ident, 1)
        pool.wait_ge(p_ident, 1)
        pool.affine_select(out=ident[:, :], in_=ident[:, :], compare_op=ALU.not_equal, fill=1.0, base=0,
                           pattern=[[-1, P]], channel_multiplier=1).then_inc(p_ident, 1)
        pool.wait_ge(p_half, 1)

        def power(dst, src, n):
            return pool.tensor_tensor(dst, src, mhalf[0:n, 0:src.shape[1]], ALU.pow)

        pool.wait_ge(v_cve, 1)
        power(crs[0:M, :], cve[0:M, :], M).then_inc(p_crs, 1)
        for t in vbd:
            pool.memset(f32(t[:, :, :, :]).rearrange("p a b c -> p (a b c)"), 0.0).then_inc(p_zero, 1)

        def may_negate(n):
            pool.wait_ge(d_mask[n.u], n.q * 16 + 16)
            v_scores.wait(pool, n.plus(-2), UT * KT - 1)

        def negative(n):
            pool.tensor_scalar(negm[:, n.u, :, :], mask_in[:, n.u, :, :], -FLT_MAX, 1.0, ALU.mult,
                               ALU.mult).then_inc(p_neg.sem, 1)

        def step(k, back=False, scores=False, front=False, norm=False, prep=None,
                 norm2=None, split=()):
            def add_projb(t):
                v = xr[:, bass.ds(k.slot(), 1), t, :]
                pool.tensor_tensor(v, v, projb[:, :].unsqueeze(1), ALU.add).then_inc(p_projb.sem, 1)

            if front:
                may_negate(k.plus(2))
            if back:
                add_projb(0)
            if front:
                negative(k.plus(2))
            if back:
                add_projb(1)
            if norm2 is not None:
                h_rstd(static(0), norm2)
            if scores:
                n = k.plus(1)
                v_max.wait(pool, n, 1)
                v = S[:, n.u, 1, :].rearrange("p (h m) -> p h m", h=H)
                pool.tensor_tensor(v, v, nmax[:, n.u, 1, :].unsqueeze(2).to_broadcast([P, H, M]),
                                   ALU.add).then_inc(p_less.sem, 1)
            if norm2 is not None:
                h_bias(static(0), norm2)
            if norm:
                n = k.plus(3)
                v_veps.wait(pool, n, 0)
                v_xhat.wait(pool, n.plus(-1), UT - 1)
                power(rstd[:, :], veps[:, :], P).then_inc(p_rstd.sem, 1)
            if scores:
                n = k.plus(1)
                for t in range(UT):
                    v_rsum.wait(pool, n, t)
                    v = S[:, n.u, t, :].rearrange("p (h m) -> p h m", h=H)
                    pool.tensor_tensor(v, v, rsum[:, n.u, t, :].unsqueeze(2).to_broadcast([P, H, M]),
                                       ALU.mult).then_inc(p_prob.sem, 1)
            if prep == "scores":
                pool.wait_ge(d_projb, 16)

        def h_rstd(n, t):
            v_hve.wait(pool, n, t)
            power(hrs[:, :], hve[:, :], P).then_inc(p_hrs.sem, 1)

        def h_bias(n, t):
            if isinstance(n.q, int) and n.q == 0 and n.u == 0 and t == 0:
                pool.wait_ge(d_fc2b, 16)
            v_hhat.wait(pool, n, t)
            v = x2[n.u][:, t, :]
            pool.tensor_tensor(v, v, fc2b[:, :], ALU.add).then_inc(p_fc2b.sem, 1)

        pipeline(pool, step)

        def step2(s, first=False, last=False):
            for j in range(JT):
                if not last and j in NORMS:
                    h_rstd(s.plus(1), NORMS.index(j))
                    h_bias(s.plus(1), NORMS.index(j))

        blocks(pool, step2)

    def scalar_program(act):
        for i in range(4, 7):
            load_row(act, i)
        act.wait_ge(d_ctx, 16)
        act.dma_start(kvw[:, :, 0:C], kv_w[:, 0:C].rearrange("(k p) n -> p k n", p=P)).then_inc(d_kw, 16)
        act.dma_start(qraw[:, :, :], q_w.rearrange("(k p) n -> p k n", p=P)).then_inc(d_qw, 16)
        act.dma_start(kvw[:, :, C:2 * C], kv_w[:, C:2 * C].rearrange("(k p) n -> p k n", p=P)).then_inc(d_vw, 16)
        act.dma_start(praw[:, :, :], proj_w.rearrange("(k p) n -> p k n", p=P)).then_inc(d_pw, 16)

        def keys_hi():
            act.wait_ge(t_keys, 1)
            act.wait_ge(v_zero, 2)
            for h2 in range(2):
                for h in range(HG):
                    r = slice(h * D, (h + 1) * D)
                    i = act.activation(kbd[HI][r, :, 2 * h2:2 * h2 + 2, h * M:(h + 1) * M].rearrange("p b g m -> p g b m"),
                                       bank[4 + h2][r, 0:4 * M].rearrange("p (g b m) -> p g b m", g=2, b=B), ACT.Copy)
            i.then_inc(a_keys, 1)

        def values_hi(b):
            act.wait_ge(t_vals, b + 1)
            act.activation(vtok[HI][0:M, b, :], bank[6 + b][0:M, :], ACT.Copy).then_inc(a_vals, 1)

        act.wait_ge(v_cols, 1)
        act.wait_ge(t_ctxT, 1)
        for k in range(KT):
            i = act.activation(cxT[:, k, 1, :], bank[3][:, k * M:(k + 1) * M], ACT.Identity,
                               bias=cols[:, CNB + k:CNB + k + 1], scale=cols[:, CNW + k:CNW + k + 1])
        i.then_inc(a_ctxT, 1)
        act.wait_ge(v_wscale, 1)
        act.wait_ge(d_qw, 16)
        for k in range(KT):
            act.activation(wq[HI][:, k, :], qraw[:, k, :], ACT.Copy, scale=wscale[:, k:k + 1]).then_inc(a_wq, 1)

        def step(k, back=False, scores=False, front=False, norm=False, prep=None,
                 norm2=None, split=()):
            b, s, f = k, k.plus(1), k.plus(2)

            def x_hi(t):
                t_xT.wait(act, f, t)
                t_q.wait(act, f.plus(-1), UT - 1)
                act.activation(xT[HI][:, :, t * P:(t + 1) * P], bA[t][:, :].rearrange("p (k n) -> p k n", k=KT),
                               ACT.Copy).then_inc(a_xT.sem, 1)

            def q_hi(h):
                t_q.wait(act, f, h)
                for m in (2 * h, 2 * h + 1):
                    i = act.activation(qT[HI][:, m, :], bA[h][:, (m % 2) * UN:(m % 2 + 1) * UN], ACT.Identity,
                                       bias=qbias[:, m:m + 1])
                i.then_inc(a_q.sem, 1)

            def prob_hi(g_):
                for t in range(UT):
                    i = g_ * UT + t
                    if t == 0:
                        t_av.wait(act, b, g_ - 2)
                    t_probT.wait(act, b, i)
                    act.activation(PT[HI][:, g_ % 2, :, t * P:(t + 1) * P],
                                   bT[i % 2][:, 0:NC * P].rearrange("p (c n) -> p c n", c=NC),
                                   ACT.Copy).then_inc(a_probT.sem, 1)

            def av_hi(g_):
                if g_ == 0:
                    t_proj.wait(act, b.plus(-1), UT - 1)
                t_av.wait(act, b, g_)
                act.activation(aT[HI][:, g_, :], bV[g_ % 2][:, 0:UN], ACT.Copy).then_inc(a_av.sem, 1)

            def exps(t, lo, hi):
                if lo == 0:
                    v_max.wait(act, s, t)
                for h in range(lo, hi):
                    v = S[:, s.u, t, h * M:(h + 1) * M]
                    i = act.activation(v, v, ACT.Exp, bias=nmax[:, s.u, t, h:h + 1],
                                       accum_out=esum[:, s.u, t, h:h + 1])
                if hi == H:
                    i.then_inc(a_exp.sem, 1)

            def exp_all(t):
                p_less.wait(act, s, 0)
                v = S[:, s.u, t, :]
                act.activation(v, v, ACT.Exp).then_inc(a_exp.sem, 1)

            if front:
                x_hi(0)
                x_hi(1)
            if prep == "q":
                keys_hi()
                act.wait_ge(d_pw, 16)
                act.activation(wp[HI][:, :, :], praw[:, :, :], ACT.Copy).then_inc(a_wp, 1)
            if split:
                w1_hi(split[0])
            if back:
                prob_hi(0)
            if scores:
                exps(0, 0, 4)
            if back:
                prob_hi(1)
            if scores:
                exps(0, 4, 6)
            if prep == "q":
                act.wait_ge(v_qbias, 1)
            if prep == "scores":
                exps(0, 6, 8)
                values_hi(0)
                exps(0, 8, 16)
                exp_all(1)
            if front:
                q_hi(0)
            if back:
                av_hi(0)
                prob_hi(2)
            if scores and prep is None:
                exps(0, 6, 10)
            if back:
                av_hi(1)
                prob_hi(3)
            if scores and prep is None:
                exps(0, 10, 12)
            if back:
                av_hi(2)
            if split:
                w1_hi(split[1])
            if scores and prep is None:
                exps(0, 12, 14)
            if front:
                q_hi(1)
            if back:
                av_hi(3)
            if scores and prep is None:
                exps(0, 14, 16)
                exp_all(1)
            if prep == "scores":
                values_hi(1)
            if norm2 is not None:
                h_hi(static(0), norm2)

        def w1_hi(j):
            act.wait_ge(d_w1[j % 2], 16 * (j // 2) + 16)
            if j == 0:
                t_q.wait(act, last_unit, UT - 1)
            if j == W1_AHEAD:
                t_proj.wait(act, last_unit, UT - 1)
            act.activation(w1[:, j, HI, :, :], w1raw[:, j % 2, :, :], ACT.Copy).then_inc(a_w1, 1)

        def w2_hi(j):
            act.wait_ge(d_w2[j % 2], 16 * (j // 2) + 16)
            if j == 0:
                t_proj.wait(act, last_unit, UT - 1)
            act.activation(w2[:, j, HI, :], w2raw[:, j % 2, :], ACT.Copy).then_inc(a_w2, 1)

        def h_hi(n, t):
            t_hT.wait(act, n, t)
            for k in range(KT):
                v = h_bank(n, t)[:, k * P:(k + 1) * P]
                i = act.activation(v, v, ACT.Identity,
                                   bias=cols[:, N2B + k:N2B + k + 1], scale=cols[:, N2W + k:N2W + k + 1])
            i.then_inc(a_hy.sem, 1)
            a_hy.wait(act, n, t)
            act.activation(hT[n.u][HI][:, :, t * P:(t + 1) * P],
                           h_bank(n, t)[:, :].rearrange("p (k n) -> p k n", k=KT), ACT.Copy).then_inc(a_hT.sem, 1)

        pipeline(act, step)

        def step2(s, first=False, last=False):
            if first:
                p_projb.wait(act, last_unit, UT - 1)
                p_neg.wait(act, last_unit, 0)
            for j in range(JT):
                t_fc1.wait(act, s, j)
                v_glo.wait(act, s, j - 1)
                act.activation(g[:, :], bF[j % 2][:, :], ACT.Gelu, bias=cols[:, F1B + j:F1B + j + 1]).then_inc(a_gelu.sem, 1)
                if first:
                    w2_hi(j)
                if first and j + W1_AHEAD < JT:
                    w1_hi(j + W1_AHEAD)
                if not last and j - 1 in NORMS:
                    h_hi(s.plus(1), NORMS.index(j - 1))

        blocks(act, step2)

    def vector_program(dve):
        for c in counts1:
            dve.sem_inc(c.sem, c.start)

        def zero_keys(part):
            dve.memset(f32(kbd[part][:, :, :, :]).rearrange("p a b c -> p (a b c)"), 0.0).then_inc(v_zero, 1)

        zero_keys(HI)
        dve.wait_ge(d_ctx, 16)
        for b in range(B):
            i = dve.bn_stats(cbn[0:M, b, :], cx[0:M, b, :])
        i.then_inc(s_chain, 1)
        dve.wait_ge(s_chain, 1)
        for b in range(B):
            i = dve.bn_aggr(cmv[0:M, b, :], cbn[0:M, b, :])
        i.then_inc(s_chain, 1)
        dve.wait_ge(s_chain, 2)
        dve.tensor_scalar(cve[0:M, :], cmv[0:M, :, 1], EPS, None, ALU.add).then_inc(v_cve, 1)
        dve.wait_ge(p_crs, 1)
        for b in range(B):
            i = dve.tensor_scalar(cx[0:M, b, :], cx[0:M, b, :], cmv[0:M, b, 0:1], crs[0:M, b:b + 1],
                                  ALU.subtract, ALU.mult)
        i.then_inc(v_ctx, 1)
        dve.wait_ge(t_cols, 1)
        dve.tensor_copy(cols[:, :], bank[7][:, 0:40]).then_inc(v_cols, 1)
        dve.wait_ge(v_cols, 1)
        dve.tensor_scalar(wscale[:, :], cols[:, QNW:QNW + KT], SCALE, None, ALU.mult).then_inc(v_wscale, 1)

        dve.wait_ge(t_ctxT, 1)
        for k in range(KT):
            i = dve.tensor_scalar(cxT[:, k, 0, :], bank[2][:, k * M:(k + 1) * M],
                                  cols[:, CNW + k:CNW + k + 1], cols[:, CNB + k:CNB + k + 1], ALU.mult, ALU.add)
        i.then_inc(v_ctxT, 1)
        zero_keys(LO)

        def q_weights():
            dve.wait_ge(v_wscale, 1)
            for k in range(KT):
                dve.wait_ge(a_wq, k + 1)
                i = dve.scalar_tensor_tensor(out=wq[LO][:, k, :], in0=qraw[:, k, :], scalar=wscale[:, k:k + 1],
                                             in1=f32(wq[HI][:, k, :]), op0=ALU.mult, op1=ALU.subtract)
            i.then_inc(v_wq, 1)

        def q_bias():
            dve.wait_ge(t_qbias, 1)
            dve.tensor_scalar(qbias[:, :], bank[2][:, 0:KT], SCALE, None, ALU.mult).then_inc(v_qbias, 1)

        def keys_lo():
            dve.wait_ge(a_keys, 1)
            for h2 in range(2):
                for h in range(HG):
                    r = slice(h * D, (h + 1) * D)
                    i = dve.tensor_tensor(*(kbd[part][r, :, 2 * h2:2 * h2 + 2, h * M:(h + 1) * M].rearrange(
                        "p b g m -> p g b m") if part == LO else
                        bank[4 + h2][r, 0:4 * M].rearrange("p (g b m) -> p g b m", g=2, b=B) for part in (LO, HI)),
                        f32(kbd[HI][r, :, 2 * h2:2 * h2 + 2, h * M:(h + 1) * M]).rearrange("p b g m -> p g b m"),
                        ALU.subtract)
            i.then_inc(v_keys, 1)

        def values_lo(b):
            dve.wait_ge(a_vals, b + 1)
            dve.tensor_tensor(vtok[LO][0:M, b, :], bank[6 + b][0:M, :], f32(vtok[HI][0:M, b, :]),
                              ALU.subtract).then_inc(v_vals, 1)

        def proj_weights():
            dve.wait_ge(a_wp, 1)
            dve.tensor_tensor(wp[LO][:, :, :], praw[:, :, :], f32(wp[HI][:, :, :]), ALU.subtract).then_inc(v_wp, 1)

        def step(k, back=False, scores=False, front=False, norm=False, prep=None,
                 norm2=None, split=()):
            b, s, f, n = k, k.plus(1), k.plus(2), k.plus(3)

            def masked(t, g_):
                i = t * KT + g_
                if i == 0:
                    p_neg.wait(dve, s, 0)
                    t_probT.wait(dve, s.plus(-2), KT * UT - 1)
                t_scores.wait(dve, s, i)
                dve.tensor_tensor(S[:, s.u, t, g_ * GM:(g_ + 1) * GM].rearrange("p (h m) -> p h m", h=HG),
                                  bS[i % 2][:, 0:GM].rearrange("p (h m) -> p h m", h=HG),
                                  negm[:, s.u, t, :].unsqueeze(1).to_broadcast([P, HG, M]),
                                  ALU.add).then_inc(v_scores.sem, 1)

            def maximum(t):
                v_scores.wait(dve, s, (t + 1) * KT - 1)
                dve.tensor_reduce(nmax[:, s.u, t, :], S[:, s.u, t, :].rearrange("p (h m) -> p h m", h=H), AX.X,
                                  ALU.max, negate=True).then_inc(v_max.sem, 1)

            def x_lo(t):
                a_xT.wait(dve, f, t)
                v = slice(t * P, (t + 1) * P)
                dve.tensor_tensor(xT[LO][:, :, v], bA[t][:, :].rearrange("p (k n) -> p k n", k=KT),
                                  f32(xT[HI][:, :, v]), ALU.subtract).then_inc(v_xT.sem, 1)

            def q_lo(h):
                a_q.wait(dve, f, h)
                for m in (2 * h, 2 * h + 1):
                    i = dve.scalar_tensor_tensor(out=qT[LO][:, m, :], in0=bA[h][:, (m % 2) * UN:(m % 2 + 1) * UN],
                                                 scalar=qbias[:, m:m + 1], in1=f32(qT[HI][:, m, :]),
                                                 op0=ALU.add, op1=ALU.subtract)
                i.then_inc(v_q.sem, 1)

            def prob_lo(g_, tiles=range(UT)):
                for t in tiles:
                    i = g_ * UT + t
                    v = slice(t * P, (t + 1) * P)
                    a_probT.wait(dve, b, i)
                    dve.tensor_tensor(PT[LO][:, g_ % 2, :, v],
                                      bT[i % 2][:, 0:NC * P].rearrange("p (c n) -> p c n", c=NC),
                                      f32(PT[HI][:, g_ % 2, :, v]), ALU.subtract).then_inc(v_probT.sem, 1)

            def av_lo(g_):
                a_av.wait(dve, b, g_)
                dve.tensor_tensor(aT[LO][:, g_, :], bV[g_ % 2][:, 0:UN], f32(aT[HI][:, g_, :]),
                                  ALU.subtract).then_inc(v_av.sem, 1)

            def exp_sum():
                a_exp.wait(dve, s, 1)
                dve.tensor_reduce(esum[:, s.u, 1, :], S[:, s.u, 1, :].rearrange("p (h m) -> p h m", h=H), AX.X,
                                  ALU.add).then_inc(v_esum.sem, 1)

            def recip(t):
                if t == 1:
                    v_esum.wait(dve, s, 0)
                else:
                    a_exp.wait(dve, s, 0)
                dve.reciprocal(rsum[:, s.u, t, :], esum[:, s.u, t, :]).then_inc(v_rsum.sem, 1)

            def stats():
                dve.wait_ge(d_x[n.u], n.q * 16 + 16)
                for t in range(UT):
                    dve.bn_stats(bnst[:, t, :], xr[:, bass.ds(n.slot(), 1), t, :]).then_inc(v_bn.sem, 1)

            def variance():
                for t in range(UT):
                    dve.bn_aggr(mv[:, t, :], bnst[:, t, :]).then_inc(v_mv.sem, 1)
                v_mv.wait(dve, n, UT - 1)
                dve.tensor_scalar(veps[:, :], mv[:, :, 1], EPS, None, ALU.add).then_inc(v_veps.sem, 1)

            def normed():
                p_rstd.wait(dve, n, 0)
                for t in range(UT):
                    t_xT.wait(dve, n.plus(-1), t)
                    dve.tensor_scalar(xhat[:, t:t + 1, :], xr[:, bass.ds(n.slot(), 1), t, :], mv[:, t, 0:1],
                                      rstd[:, t:t + 1], ALU.subtract, ALU.mult).then_inc(v_xhat.sem, 1)

            def residual(t):
                t_proj.wait(dve, b, t)
                p_projb.wait(dve, b, t)
                v = xr[:, bass.ds(b.slot(), 1), t, :]
                dve.tensor_tensor(v, bV[t][:, :].unsqueeze(1), v, ALU.add).then_inc(v_res.sem, 1)

            if prep == "q":
                q_weights()
            if scores:
                masked(0, 0)
                masked(0, 1)
            if front and prep != "scores":
                x_lo(0)
                x_lo(1)
            if norm2 is not None:
                h_stats(static(0), norm2)
            if split:
                w1_lo(split[0])
            if prep == "q":
                stats()
                v_bn.wait(dve, n, UT - 1)
                variance()
                keys_lo()
                q_bias()
                normed()
                proj_weights()
            if scores:
                masked(0, 2)
                masked(0, 3)
            if back:
                prob_lo(0, (0,))
            if scores and prep is None:
                maximum(0)
            if norm2 is not None:
                v_hbn.wait(dve, static(0), norm2)
                h_variance(static(0), norm2)
            if back:
                prob_lo(0, (1,))
            if scores:
                masked(1, 0)
                masked(1, 1)
            if back:
                prob_lo(1)
            if scores:
                masked(1, 2)
                masked(1, 3)
            if prep == "scores":
                maximum(0)
                x_lo(0)
                x_lo(1)
            if scores:
                maximum(1)
            if prep == "scores":
                stats()
                v_bn.wait(dve, n, UT - 1)
                variance()
                values_lo(0)
                recip(0)
                exp_sum()
                recip(1)
            if back:
                av_lo(0)
                prob_lo(2)
            if front:
                q_lo(0)
            if back:
                av_lo(1)
                prob_lo(3)
            if norm2 is not None:
                h_normed(static(0), norm2)
            if norm and prep is None:
                stats()
                v_bn.wait(dve, n, UT - 1)
            if back:
                av_lo(2)
            if split:
                w1_lo(split[1])
            if norm and prep is None:
                variance()
            if front:
                q_lo(1)
            if back:
                av_lo(3)
            if scores and prep is None:
                recip(0)
            if norm and prep != "q":
                normed()
            if prep == "scores":
                values_lo(1)
            if scores and prep is None:
                exp_sum()
                recip(1)
            if back:
                residual(0)
            if norm2 is not None:
                h_lo(static(0), norm2)
            if back:
                residual(1)

        def w1_lo(j):
            dve.wait_ge(a_w1, j + 1)
            dve.tensor_tensor(w1[:, j, LO, :, :], w1raw[:, j % 2, :, :], f32(w1[:, j, HI, :, :]),
                              ALU.subtract).then_inc(v_w1, 1)

        def w2_lo(j):
            dve.wait_ge(a_w2, j + 1)
            dve.tensor_tensor(w2[:, j, LO, :], w2raw[:, j % 2, :], f32(w2[:, j, HI, :]),
                              ALU.subtract).then_inc(v_w2, 1)

        def h_stats(n, t):
            if t == 0:
                dve.wait_ge(d_x2[n.u], n.q * 16 + 16)
            dve.bn_stats(hbn[:, :], x2[n.u][:, t, :]).then_inc(v_hbn.sem, 1)

        def h_variance(n, t):
            dve.bn_aggr(hmv[:, :], hbn[:, :]).then_inc(v_hmv.sem, 1)
            v_hmv.wait(dve, n, t)
            dve.tensor_scalar(hve[:, :], hmv[:, 1:2], EPS, None, ALU.add).then_inc(v_hve.sem, 1)

        def h_normed(n, t):
            p_hrs.wait(dve, n, t)
            t_hT.wait(dve, n, t - 1)
            dve.tensor_scalar(hhat[:, :], x2[n.u][:, t, :], hmv[:, 0:1], hrs[:, 0:1], ALU.subtract,
                              ALU.mult).then_inc(v_hhat.sem, 1)

        def h_norm(n, t):
            h_stats(n, t)
            v_hbn.wait(dve, n, t)
            h_variance(n, t)
            h_normed(n, t)

        def h_lo(n, t):
            a_hT.wait(dve, n, t)
            v = slice(t * P, (t + 1) * P)
            dve.tensor_tensor(hT[n.u][LO][:, :, v], h_bank(n, t)[:, :].rearrange("p (k n) -> p k n", k=KT), f32(hT[n.u][HI][:, :, v]), ALU.subtract).then_inc(v_hT.sem, 1)

        pipeline(dve, step)

        def step2(s, first=False, last=False):
            def output(n, t):
                t_fc2.wait(dve, n, (JT - 1) * ST + t)
                p_fc2b.wait(dve, n, t)
                dve.tensor_tensor(x2[n.u][:, t, :], bC[t][:, :], x2[n.u][:, t, :], ALU.add).then_inc(v_out.sem, 1)

            for j in range(JT):
                a_gelu.wait(dve, s, j)
                t_fc2.wait(dve, s, (j - 3) * ST - 1)
                dve.tensor_copy(gT[HI][:, j % 4, :], g[:, :]).then_inc(v_ghi.sem, 1)
                norming = not last and j in NORMS
                if norming:
                    h_stats(s.plus(1), NORMS.index(j))
                    v_hbn.wait(dve, s.plus(1), NORMS.index(j))
                v_ghi.wait(dve, s, j)
                dve.tensor_tensor(gT[LO][:, j % 4, :], g[:, :], f32(gT[HI][:, j % 4, :]),
                                  ALU.subtract).then_inc(v_glo.sem, 1)
                if first:
                    w2_lo(j)
                if first and j + W1_AHEAD < JT:
                    w1_lo(j + W1_AHEAD)
                if not first and j == 1:
                    for t in range(ST):
                        output(s.plus(-1), t)
                if not last and j - 2 in NORMS:
                    h_lo(s.plus(1), NORMS.index(j - 2))
                if norming:
                    h_variance(s.plus(1), NORMS.index(j))
                    h_normed(s.plus(1), NORMS.index(j))
            if last:
                for t in range(ST):
                    output(s, t)

        blocks(dve, step2)

    def tensor_program(pe):
        pe.wait_ge(p_ident, 2)
        pe.wait_ge(v_ctx, 1)
        for b in range(B):
            for k in range(KT):
                i = pe.transpose(bank[2 + b][:, k * M:(k + 1) * M], cx[0:M, b, k * P:(k + 1) * P], ident[0:M, 0:M])
        i.then_inc(t_ctxT, 1)
        pe.wait_ge(d_rows, 16 * 7)
        pe.transpose(bank[7][:, 0:40], rows[:, :], ident[0:40, 0:40]).then_inc(t_cols, 1)

        def q_bias():
            pe.wait_ge(v_cols, 1)
            pe.wait_ge(d_qw, 16)
            for m in range(KT):
                for k in range(KT):
                    i = pe.matmul(bank[2][:, m:m + 1], qraw[:, k, m * P:(m + 1) * P], cols[:, QNB + k:QNB + k + 1],
                                  start=(k == 0), stop=(k == KT - 1))
            i.then_inc(t_qbias, 1)

        def keys():
            pe.wait_ge(v_ctxT, 1)
            pe.wait_ge(a_ctxT, 1)
            pe.wait_ge(d_kw, 16)
            for g_ in range(KT):
                for k in range(KT):
                    i = pe.matmul(bank[4 + g_ // 2][:, (g_ % 2) * B * M:(g_ % 2 + 1) * B * M],
                                  kvw[:, k, g_ * P:(g_ + 1) * P], cxT[:, k, :, :].rearrange("p b m -> p (b m)"),
                                  start=(k == 0), stop=(k == KT - 1))
            i.then_inc(t_keys, 1)

        def values(b):
            pe.wait_ge(d_vw, 16)
            for k in range(KT):
                i = pe.matmul(bank[6 + b][0:M, :], cxT[:, k, b, :], kvw[:, k, C:2 * C],
                              start=(k == 0), stop=(k == KT - 1))
            i.then_inc(t_vals, 1)

        def step(k, back=False, scores=False, front=False, norm=False, prep=None,
                 norm2=None, split=()):
            b, s, f = k, k.plus(1), k.plus(2)

            def score(t, g_):
                i = t * KT + g_
                if i == 0:
                    v_q.wait(pe, s, UT - 1)
                v_scores.wait(pe, s, i - 2)
                for n, (w, d) in enumerate(PRODUCTS):
                    mm = pe.matmul(bS[i % 2][:, 0:GM], qT[d][:, g_, t * P:(t + 1) * P], kbd[w][:, s.u, g_, :],
                                   start=(n == 0), stop=(n == 2))
                mm.then_inc(t_scores.sem, 1)

            def x_T(t):
                v_xhat.wait(pe, f, t)
                v_q.wait(pe, f.plus(-1), t)
                if t == 0 and norm2:
                    v_hT.wait(pe, static(0), norm2 - 1)
                for c in range(KT):
                    mm = pe.transpose(bA[t][:, c * P:(c + 1) * P], xhat[:, t, c * P:(c + 1) * P], ident[:, :])
                mm.then_inc(t_xT.sem, 1)

            def q(m):
                if m == 0:
                    v_xT.wait(pe, f, UT - 1)
                n = 0
                for c in range(KT):
                    for w, d in PRODUCTS:
                        mm = pe.matmul(bA[m // 2][:, (m % 2) * UN:(m % 2 + 1) * UN], wq[w][:, c, m * P:(m + 1) * P],
                                       xT[d][:, c, :], start=(n == 0), stop=(n == 3 * KT - 1))
                        n += 1
                if m % 2:
                    mm.then_inc(t_q.sem, 1)

            def prob_T1(g_, t):
                i = g_ * UT + t
                if i == 0:
                    p_prob.wait(pe, b, UT - 1)
                v_probT.wait(pe, b, i - 2)
                for c in range(NC):
                    r = g_ * GM + CH0[c]
                    mm = pe.transpose(bT[i % 2][:, c * P:(c + 1) * P], S[:, b.u, t, r:r + P], ident[:, :])
                mm.then_inc(t_probT.sem, 1)

            def prob_T(g_):
                for t in range(UT):
                    prob_T1(g_, t)

            def av(g_):
                if g_ == 0:
                    pe.wait_ge(d_vbd[b.u], 16 * 12)
                v_probT.wait(pe, b, g_ * UT + UT - 1)
                if g_ < 2:
                    v_res.wait(pe, b.plus(-1), g_)
                else:
                    v_av.wait(pe, b, g_ - 2)
                n = 0
                for c in range(NC):
                    for w, d in PRODUCTS:
                        mm = pe.matmul(bV[g_ % 2][:, 0:UN], vbd[w][:, b.u, g_ * NC + c, :], PT[d][:, g_ % 2, c, :],
                                       start=(n == 0), stop=(n == 3 * NC - 1))
                        n += 1
                mm.then_inc(t_av.sem, 1)

            def proj(t):
                n = 0
                for c in range(KT):
                    if t == 0 and c in (0, KT - 1):
                        v_av.wait(pe, b, KT - 2 + (c > 0))
                    for w, d in PRODUCTS:
                        mm = pe.matmul(bV[t][:, :], aT[d][:, c, t * P:(t + 1) * P], wp[w][:, c, :],
                                       start=(n == 0), stop=(n == 3 * KT - 1))
                        n += 1
                mm.then_inc(t_proj.sem, 1)

            if prep == "q":
                keys()
                x_T(0)
                x_T(1)
                q_bias()
                pe.wait_ge(v_wq, 1)
            elif prep == "scores":
                x_T(0)
                x_T(1)
                pe.wait_ge(v_keys, 1)
                for t in range(UT):
                    for g_ in range(KT):
                        score(t, g_)
                values(0)
            if split and not scores:
                fc1(static(0), 1, first=True, parts=(0, 1))
            if scores and prep is None:
                score(0, 0)
            if front and prep is None:
                x_T(0)
            if scores and prep is None:
                score(0, 1)
            if front and prep is None:
                x_T(1)
            if back:
                prob_T1(0, 0)
            if scores and prep is None:
                score(0, 2)
            if back:
                prob_T1(0, 1)
            if scores and prep is None:
                score(0, 3)
            if split and scores:
                fc1(static(0), 0, first=True, parts=(0, 1))
            elif split:
                fc1(static(0), 1, parts=(2, 3))
            if front:
                q(0)
            if scores and prep is None:
                score(1, 0)
                score(1, 1)
            if front:
                q(1)
            if back:
                prob_T(1)
            if scores and prep is None:
                score(1, 2)
                score(1, 3)
            if split and scores:
                fc1(static(0), 0, parts=(2, 3))
            if back:
                av(0)
                prob_T(2)
            if front:
                q(2)
            if back:
                av(1)
                prob_T(3)
            if back:
                av(2)
            if front:
                q(3)
            if prep == "scores":
                values(1)
            if back:
                av(3)
            if norm2 is not None:
                h_T(static(0), norm2)
            if back:
                proj(0)
                proj(1)

        def fc1(s, j, first=False, parts=range(KT)):
            if first:
                pe.wait_ge(v_w1, j + 1)
            if j == 0 and parts[0] == 0:
                v_hT.wait(pe, s, ST - 1)
            if first and j == 1:
                v_q.wait(pe, last_unit, 1)
            if parts[0] == 0:
                a_gelu.wait(pe, s, j - 2)
            for c in parts:
                for i, (w, d) in enumerate(PRODUCTS):
                    mm = pe.matmul(bF[j % 2][:, :], w1[:, j, w, c, :], hT[s.u][d][:, c, :],
                                   start=(c == 0 and i == 0), stop=(c == KT - 1 and i == 2))
            if parts[-1] == KT - 1:
                mm.then_inc(t_fc1.sem, 1)

        def h_T(n, t):
            v_hhat.wait(pe, n, t)
            if h_bank(n, t) is bX:
                v_hT.wait(pe, n, t - 1)
            else:
                v_q.wait(pe, static(NU - 4 + t), 0)
            for c in range(KT):
                mm = pe.transpose(h_bank(n, t)[:, c * P:(c + 1) * P], hhat[:, c * P:(c + 1) * P], ident[:, :])
            mm.then_inc(t_hT.sem, 1)

        pipeline(pe, step)

        def step2(s, first=False, last=False):
            def fc2(n, j):
                if first:
                    pe.wait_ge(v_w2, j + 1)
                v_glo.wait(pe, n, j)
                for t in range(ST):
                    if first and j == 0 and t == 0:
                        v_res.wait(pe, last_unit, UT - 1)
                    if j == 0:
                        v_out.wait(pe, n.plus(-1), t)
                    for i, (w, d) in enumerate(PRODUCTS):
                        mm = pe.matmul(bC[t][:, :], gT[d][:, j % 4, t * P:(t + 1) * P], w2[:, j, w, :],
                                       start=(j == 0 and i == 0), stop=(j == JT - 1 and i == 2))
                    mm.then_inc(t_fc2.sem, 1)

            for j in range(JT):
                if not first or j >= 2:
                    fc1(s, j, first)
                if j >= 2:
                    fc2(s, j - 2)
                elif not first:
                    fc2(s.plus(-1), JT - 2 + j)
                if not last and j - 1 in NORMS:
                    h_T(s.plus(1), NORMS.index(j - 1))
            if first:
                pe.wait_ge(v_w2, JT)
            if last:
                fc2(s, JT - 2)
                fc2(s, JT - 1)

        blocks(pe, step2)

    with nc.Block() as block:
        block.sync(sync_program)
        block.gpsimd(gpsimd_program)
        block.scalar(scalar_program)
        block.vector(vector_program)
        block.tensor(tensor_program)


INPUTS = ["x", "ctx_1024", "mask_BxSxS2_bk0"] + [
    f"L0_xattn_{n}" for n in ("qn_w", "qn_b", "cn_w", "cn_b", "n2_w", "n2_b", "q_w", "kv_w", "proj_w", "proj_b",
                              "fc1_w", "fc1_b", "fc2_w", "fc2_b")]


def kernel(**inputs):
    import numpy as np
    import concourse.bacc as bacc
    from concourse.bass_utils import run_bass_kernel_spmd

    nc = bacc.Bacc("TRN2", target_bir_lowering=False, num_devices=1)
    arrays, args = {}, []
    for name in INPUTS:
        a = np.ascontiguousarray(inputs[name])
        arrays[f"in_{name}"] = a
        args.append(nc.dram_tensor(f"in_{name}", a.shape, mybir.dt.from_np(a.dtype), kind="ExternalInput").ap())
    args.append(nc.dram_tensor("out_0", inputs["x"].shape, F32, kind="ExternalOutput").ap())
    build_block(nc, *args)
    return run_bass_kernel_spmd(nc, [arrays], core_ids=[0]).results[0]["out_0"]
```
